# Optimizing a Trainium2 kernel written in Bass

```python
import numpy as np
import jax
import jax.numpy as jnp

def _softmax(x, axis=-1):
    return jax.nn.softmax(x, axis=axis)

def _gelu(x):
    return jax.nn.gelu(x, approximate=True)

def _silu(x):
    return jax.nn.silu(x)

def _sigmoid(x):
    return jax.nn.sigmoid(x)

def _layernorm(x, axis=-1, eps=1e-05):
    m = jnp.mean(x, axis=axis, keepdims=True)
    v = jnp.var(x, axis=axis, keepdims=True)
    return (x - m) / jnp.sqrt(v + eps)

def _scatter_add(tgt, idx, src, axis=0):
    return tgt.at[idx].add(src)

def _segment_sum(src, seg, n):
    return jax.ops.segment_sum(src, seg, n)
kernel_name = 'mk_vit_tower_d1_tok_img768_r4_faa3a1'

def setup_inputs(seed: int=0):
    np.random.seed(seed)
    _w = jnp.asarray

    def _rec_inputs():
        import jax
        import jax.numpy as jnp
        _rk = jax.random.key(seed)
        x = -1.80045e-05 + 0.999906 * jax.random.normal(jax.random.fold_in(_rk, 1), (64, 3, 96, 96), jnp.float32)
        return x
    x = _rec_inputs()

    def _L0_tok_setup():
        import jax, jax.numpy as jnp
        import numpy as np
        IMAGE_SIZE = 96
        PATCH = 16
        CHANNELS = 3
        TOKEN_DIM = 192
        NUM_PATCHES = (IMAGE_SIZE // PATCH) ** 2
        PATCH_DIM = CHANNELS * PATCH * PATCH
        N_TOKENS = NUM_PATCHES + 1

        def _fixed_pos_embedding(n_tokens, dim):
            i = np.arange(n_tokens, dtype=np.float32)[:, None]
            j = np.arange(dim, dtype=np.float32)[None, :]
            j_even = np.where(j % 2 == 0, j, j - 1)
            angle = i / np.power(10000.0, j_even / dim)
            tab = np.where(j % 2 == 0, np.sin(angle), np.cos(angle)).astype(np.float32)
            return jnp.asarray(tab)

        def _make_patches(image):
            B, C, H, Wd = image.shape
            p = PATCH
            hp, wp = (H // p, Wd // p)
            x = image.reshape(B, C, hp, p, wp, p)
            x = x.transpose(0, 1, 2, 4, 3, 5)
            return x.reshape(B, hp * wp, C * p * p)
        key = jax.random.key(seed)
        k_img, k_w, k_b, k_cls = jax.random.split(key, 4)
        image = jax.random.normal(k_img, (128, CHANNELS, IMAGE_SIZE, IMAGE_SIZE), dtype=jnp.float32)
        W = jax.random.normal(k_w, (TOKEN_DIM, PATCH_DIM), dtype=jnp.float32) / np.sqrt(PATCH_DIM)
        b = jax.random.normal(k_b, (TOKEN_DIM,), dtype=jnp.float32) * 0.01
        class_token = jax.random.normal(k_cls, (1, TOKEN_DIM), dtype=jnp.float32)
        pos_embedding = _fixed_pos_embedding(N_TOKENS, TOKEN_DIM)
        return {'image': image, 'W': W, 'b': b, 'class_token': class_token, 'pos_embedding': pos_embedding}
    _L0_tok_all = _L0_tok_setup()
    _L0_tok_in = {k: v for k, v in _L0_tok_all.items() if k in ('W', 'b', 'class_token', 'pos_embedding')}
    del _L0_tok_all

    def _L0_attn_setup():
        import jax, jax.numpy as jnp
        import numpy as np
        N_HEADS = 12
        HIDDEN = 192
        HEAD_DIM = HIDDEN // N_HEADS
        B, S = (4, 512)
        key = jax.random.key(seed)
        ks = jax.random.split(key, 7)
        bound = 1.0 / np.sqrt(HIDDEN)
        inputs = jax.random.normal(ks[0], (B, S, HIDDEN), dtype=jnp.float32)
        Wq = jax.random.uniform(ks[1], (HIDDEN, HIDDEN), jnp.float32, -bound, bound)
        bq = jax.random.uniform(ks[2], (HIDDEN,), jnp.float32, -bound, bound)
        Wk = jax.random.uniform(ks[3], (HIDDEN, HIDDEN), jnp.float32, -bound, bound)
        bk = jax.random.uniform(ks[4], (HIDDEN,), jnp.float32, -bound, bound)
        Wv = jax.random.uniform(ks[5], (HIDDEN, HIDDEN), jnp.float32, -bound, bound)
        bv = jax.random.uniform(ks[6], (HIDDEN,), jnp.float32, -bound, bound)
        return {'inputs': inputs, 'Wq': Wq, 'bq': bq, 'Wk': Wk, 'bk': bk, 'Wv': Wv, 'bv': bv}
    _L0_attn_all = _L0_attn_setup()
    _L0_attn_in = {k: v for k, v in _L0_attn_all.items() if k in ('Wq', 'bq', 'Wk', 'bk', 'Wv', 'bv')}
    del _L0_attn_all

    def _L0_ffn_setup():
        import jax, jax.numpy as jnp
        import numpy as np
        DIM = 192
        HEADS = 12
        EXPERTS = 8
        HID = 768
        TOP_K = 2
        LN_EPS = 1e-05

        def _layer_norm(x, g, b):
            mu = x.mean(-1, keepdims=True)
            var = ((x - mu) ** 2).mean(-1, keepdims=True)
            return (x - mu) * jax.lax.rsqrt(var + LN_EPS) * g + b

        def _attention(x, qkv_w, qkv_b, proj_w, proj_b):
            B, N, C = x.shape
            hd = C // HEADS
            qkv = (x @ qkv_w + qkv_b).reshape(B, N, 3, HEADS, hd).transpose(2, 0, 3, 1, 4)
            q, k, v = (qkv[0], qkv[1], qkv[2])
            attn = jax.nn.softmax(jnp.einsum('bhnd,bhmd->bhnm', q, k) * hd ** (-0.5), axis=-1)
            o = jnp.einsum('bhnm,bhmd->bhnd', attn, v).transpose(0, 2, 1, 3).reshape(B, N, C)
            return o @ proj_w + proj_b

        def _moe_mlp(xn, gate_w, w1, b1, w2, b2):
            T = xn.shape[0]
            logits = xn @ gate_w
            top_logits, top_idx = jax.lax.top_k(logits, TOP_K)
            top_gates = jax.nn.softmax(top_logits, axis=-1)
            gates = jnp.zeros((T, EXPERTS), xn.dtype).at[jnp.arange(T)[:, None], top_idx].set(top_gates)
            h = jax.nn.gelu(jnp.einsum('td,edh->teh', xn, w1) + b1, approximate=False)
            y = jnp.einsum('teh,ehd->ted', h, w2) + b2
            return jnp.einsum('ted,te->td', y, gates)
        key = jax.random.key(seed)
        ks = jax.random.split(key, 16)
        s = 0.02
        return {'x': jax.random.normal(ks[0], (8, 196, DIM), jnp.float32), 'ln1_g': jnp.ones((DIM,), jnp.float32), 'ln1_b': jnp.zeros((DIM,), jnp.float32), 'qkv_w': jax.random.normal(ks[1], (DIM, 3 * DIM), jnp.float32) * s, 'qkv_b': jnp.zeros((3 * DIM,), jnp.float32), 'proj_w': jax.random.normal(ks[2], (DIM, DIM), jnp.float32) * s, 'proj_b': jnp.zeros((DIM,), jnp.float32), 'ln2_g': jnp.ones((DIM,), jnp.float32), 'ln2_b': jnp.zeros((DIM,), jnp.float32), 'gate_w': jax.random.normal(ks[3], (DIM, EXPERTS), jnp.float32) * s, 'w1': jax.random.normal(ks[4], (EXPERTS, DIM, HID), jnp.float32) * s, 'b1': jnp.zeros((EXPERTS, HID), jnp.float32), 'w2': jax.random.normal(ks[5], (EXPERTS, HID, DIM), jnp.float32) * s, 'b2': jnp.zeros((EXPERTS, DIM), jnp.float32)}
    _L0_ffn_all = _L0_ffn_setup()
    _L0_ffn_in = {k: v for k, v in _L0_ffn_all.items() if k in ('ln1_g', 'ln1_b', 'qkv_w', 'qkv_b', 'proj_w', 'proj_b', 'ln2_g', 'ln2_b', 'gate_w', 'w1', 'b1', 'w2', 'b2')}
    del _L0_ffn_all
    return {'x': x, 'L0_tok_W': _L0_tok_in['W'], 'L0_tok_b': _L0_tok_in['b'], 'L0_tok_class_token': _L0_tok_in['class_token'], 'L0_tok_pos_embedding': _L0_tok_in['pos_embedding'], 'L0_attn_Wq': _L0_attn_in['Wq'], 'L0_attn_bq': _L0_attn_in['bq'], 'L0_attn_Wk': _L0_attn_in['Wk'], 'L0_attn_bk': _L0_attn_in['bk'], 'L0_attn_Wv': _L0_attn_in['Wv'], 'L0_attn_bv': _L0_attn_in['bv'], 'L0_ffn_ln1_g': _L0_ffn_in['ln1_g'], 'L0_ffn_ln1_b': _L0_ffn_in['ln1_b'], 'L0_ffn_qkv_w': _L0_ffn_in['qkv_w'], 'L0_ffn_qkv_b': _L0_ffn_in['qkv_b'], 'L0_ffn_proj_w': _L0_ffn_in['proj_w'], 'L0_ffn_proj_b': _L0_ffn_in['proj_b'], 'L0_ffn_ln2_g': _L0_ffn_in['ln2_g'], 'L0_ffn_ln2_b': _L0_ffn_in['ln2_b'], 'L0_ffn_gate_w': _L0_ffn_in['gate_w'], 'L0_ffn_w1': _L0_ffn_in['w1'], 'L0_ffn_b1': _L0_ffn_in['b1'], 'L0_ffn_w2': _L0_ffn_in['w2'], 'L0_ffn_b2': _L0_ffn_in['b2']}

def reference(x, L0_tok_W, L0_tok_b, L0_tok_class_token, L0_tok_pos_embedding, L0_attn_Wq, L0_attn_bq, L0_attn_Wk, L0_attn_bk, L0_attn_Wv, L0_attn_bv, L0_ffn_ln1_g, L0_ffn_ln1_b, L0_ffn_qkv_w, L0_ffn_qkv_b, L0_ffn_proj_w, L0_ffn_proj_b, L0_ffn_ln2_g, L0_ffn_ln2_b, L0_ffn_gate_w, L0_ffn_w1, L0_ffn_b1, L0_ffn_w2, L0_ffn_b2):
    import jax
    import jax.numpy as jnp

    def _L0_tok_ref(image, W, b, class_token, pos_embedding):
        import jax, jax.numpy as jnp
        import numpy as np
        IMAGE_SIZE = 96
        PATCH = 16
        CHANNELS = 3
        TOKEN_DIM = 192
        NUM_PATCHES = (IMAGE_SIZE // PATCH) ** 2
        PATCH_DIM = CHANNELS * PATCH * PATCH
        N_TOKENS = NUM_PATCHES + 1

        def _fixed_pos_embedding(n_tokens, dim):
            i = np.arange(n_tokens, dtype=np.float32)[:, None]
            j = np.arange(dim, dtype=np.float32)[None, :]
            j_even = np.where(j % 2 == 0, j, j - 1)
            angle = i / np.power(10000.0, j_even / dim)
            tab = np.where(j % 2 == 0, np.sin(angle), np.cos(angle)).astype(np.float32)
            return jnp.asarray(tab)

        def _make_patches(image):
            B, C, H, Wd = image.shape
            p = PATCH
            hp, wp = (H // p, Wd // p)
            x = image.reshape(B, C, hp, p, wp, p)
            x = x.transpose(0, 1, 2, 4, 3, 5)
            return x.reshape(B, hp * wp, C * p * p)
        patches = _make_patches(image)
        tokens = jnp.einsum('bnd,td->bnt', patches, W) + b
        B = tokens.shape[0]
        cls = jnp.broadcast_to(class_token[None, :, :], (B, 1, TOKEN_DIM))
        tokens = jnp.concatenate([cls, tokens], axis=1)
        return tokens + pos_embedding[None, :, :]

    def _L0_attn_ref(inputs, Wq, bq, Wk, bk, Wv, bv):
        import jax, jax.numpy as jnp
        import numpy as np
        N_HEADS = 12
        HIDDEN = 192
        HEAD_DIM = HIDDEN // N_HEADS
        B, S = (4, 512)
        b, s, d = inputs.shape
        h, hd = (N_HEADS, HEAD_DIM)

        def proj(W, bias):
            y = inputs @ W.T + bias
            return y.reshape(b, s, h, hd).transpose(0, 2, 1, 3)
        q = proj(Wq, bq)
        k = proj(Wk, bk)
        v = proj(Wv, bv)
        scale = 1.0 / jnp.sqrt(jnp.asarray(hd, inputs.dtype))
        scores = jnp.einsum('bhqd,bhkd->bhqk', q, k) * scale
        attn = jax.nn.softmax(scores, axis=-1)
        out = jnp.einsum('bhqk,bhkd->bhqd', attn, v)
        return out.transpose(0, 2, 1, 3).reshape(b, s, d)

    def _L0_ffn_ref(x, ln1_g, ln1_b, qkv_w, qkv_b, proj_w, proj_b, ln2_g, ln2_b, gate_w, w1, b1, w2, b2):
        import jax, jax.numpy as jnp
        import numpy as np
        DIM = 192
        HEADS = 12
        EXPERTS = 8
        HID = 768
        TOP_K = 2
        LN_EPS = 1e-05

        def _layer_norm(x, g, b):
            mu = x.mean(-1, keepdims=True)
            var = ((x - mu) ** 2).mean(-1, keepdims=True)
            return (x - mu) * jax.lax.rsqrt(var + LN_EPS) * g + b

        def _attention(x, qkv_w, qkv_b, proj_w, proj_b):
            B, N, C = x.shape
            hd = C // HEADS
            qkv = (x @ qkv_w + qkv_b).reshape(B, N, 3, HEADS, hd).transpose(2, 0, 3, 1, 4)
            q, k, v = (qkv[0], qkv[1], qkv[2])
            attn = jax.nn.softmax(jnp.einsum('bhnd,bhmd->bhnm', q, k) * hd ** (-0.5), axis=-1)
            o = jnp.einsum('bhnm,bhmd->bhnd', attn, v).transpose(0, 2, 1, 3).reshape(B, N, C)
            return o @ proj_w + proj_b

        def _moe_mlp(xn, gate_w, w1, b1, w2, b2):
            T = xn.shape[0]
            logits = xn @ gate_w
            top_logits, top_idx = jax.lax.top_k(logits, TOP_K)
            top_gates = jax.nn.softmax(top_logits, axis=-1)
            gates = jnp.zeros((T, EXPERTS), xn.dtype).at[jnp.arange(T)[:, None], top_idx].set(top_gates)
            h = jax.nn.gelu(jnp.einsum('td,edh->teh', xn, w1) + b1, approximate=False)
            y = jnp.einsum('teh,ehd->ted', h, w2) + b2
            return jnp.einsum('ted,te->td', y, gates)
        B, N, C = x.shape
        x = x + _attention(_layer_norm(x, ln1_g, ln1_b), qkv_w, qkv_b, proj_w, proj_b)
        xn = _layer_norm(x, ln2_g, ln2_b).reshape(B * N, C)
        moe_out = _moe_mlp(xn, gate_w, w1, b1, w2, b2).reshape(B, N, C)
        return x + moe_out
    h = _L0_tok_ref(x, L0_tok_W, L0_tok_b, L0_tok_class_token, L0_tok_pos_embedding)
    h = h + _L0_attn_ref(_layernorm(h, axis=-1), L0_attn_Wq, L0_attn_bq, L0_attn_Wk, L0_attn_bk, L0_attn_Wv, L0_attn_bv)
    h = h + _L0_ffn_ref(_layernorm(h, axis=-1), L0_ffn_ln1_g, L0_ffn_ln1_b, L0_ffn_qkv_w, L0_ffn_qkv_b, L0_ffn_proj_w, L0_ffn_proj_b, L0_ffn_ln2_g, L0_ffn_ln2_b, L0_ffn_gate_w, L0_ffn_w1, L0_ffn_b1, L0_ffn_w2, L0_ffn_b2)
    return h

_drawn_inputs = setup_inputs


def setup_inputs(seed=0):
    import zlib

    import numpy as np

    out = dict(_drawn_inputs(seed))
    spreads = {'L0_ffn_ln1_g': (1.0, 0.6),
     'L0_ffn_ln1_b': (0.0, 0.8),
     'L0_ffn_qkv_b': (0.0, 0.488),
     'L0_ffn_proj_b': (0.0, 0.1),
     'L0_ffn_ln2_g': (1.0, 0.6),
     'L0_ffn_ln2_b': (0.0, 0.667),
     'L0_ffn_b1': (0.0, 0.8),
     'L0_ffn_b2': (0.0, 0.1)}
    factors = {'L0_tok_b': 5.802, 'L0_attn_bq': 25.726, 'L0_attn_bk': 64.0, 'L0_ffn_qkv_w': 3.041}
    for name, (base, spread) in spreads.items():
        noise = np.random.default_rng([zlib.crc32(name.encode()), seed]).standard_normal(out[name].shape)
        drawn = base * np.exp(spread * noise) if base else spread * noise
        out[name] = jnp.asarray(drawn.astype(out[name].dtype))
    for name, factor in factors.items():
        out[name] = (out[name] * factor).astype(out[name].dtype)
    return out
```

```python
import numpy as np
import concourse.bass as bass
from concourse import mybir
from contextlib import ExitStack

IMAGES, CHANNELS, SIDE, PATCH = 64, 3, 96, 16
PER_SIDE = SIDE // PATCH
PATCHES = PER_SIDE * PER_SIDE
TOK = PATCHES + 1
DIM, HEADS = 192, 12
HD = DIM // HEADS
EXPERTS, HID = 8, 768
PIX = CHANNELS * PATCH * PATCH
P = 128
TI = 3
TT = TI * TOK
NT = -(-IMAGES // TI)
TAIL = (IMAGES - (NT - 1) * TI) * TOK
GT = 2
NG = NT // GT
KC = PIX // P
D1 = DIM - P
AUG = D1 + 4
SLOT = 32
SH = P // SLOT
MT = HEADS // SH
VW = HD + 1
BIG = float(2 ** 40)
EPS = 1e-5
RSTD_OPS = 8
HC = HID // P
BT = 2
BLK = BT * TT
NB = NT // BT


def inside(t, off):
    return not isinstance(t, int) or 0 <= t + off < NT


def build(nc, x, pos, tok_b, cls, w_emb, wqk_a, wqk_b, wv_a, wv_b, ln1, ln2, proj, gate, w1, b1, w2, b2,
          ident_in, aug_in, iota_in, out):
    f32 = mybir.dt.float32
    u32 = mybir.dt.uint32
    ALU, ACT, AX = mybir.AluOpType, mybir.ActivationFunctionType, mybir.AxisListType.X
    ctx = ExitStack()
    with ctx:
        def sb(name, shape, dt=f32):
            return ctx.enter_context(nc.sbuf_tensor(name, shape, dt))

        def sem(name):
            return ctx.enter_context(nc.semaphore(name))

        ident = sb("ident", [P, P])
        posb = sb("posb", [TT, DIM])
        bias_cls = sb("bias_cls", [TT, DIM])
        wemb = sb("wemb", [P, KC, DIM])
        wqka = sb("wqka", [P, 2, 2 * MT * P])
        wqkb = sb("wqkb", [AUG, 2, 2 * MT * P])
        wva = sb("wva", [P, 2, HEADS * VW])
        wvb = sb("wvb", [AUG, 2, HEADS * VW])
        lnw = sb("lnw", [P, 2, 4])
        projw = sb("projw", [P, 2, DIM])
        gatew = sb("gatew", [P, 2, EXPERTS])
        b2s = sb("b2s", [AUG, 2, DIM])
        iota = sb("iota", [TT, NT, EXPERTS])
        patches = sb("patches", [P, 2, GT, KC, TT])
        h = sb("h", [TT, NT, DIM])
        xall = sb("xall", [TT, NT, DIM])
        oall = sb("oall", [TT, NT, DIM])
        stats = sb("stats", [TT, 4, NT, 2, 3])
        mean = sb("mean", [TT, 4, NT])
        rstd = sb("rstd", [TT, 4, NT])
        gap = sb("gap", [TT, NT])
        half = sb("half", [TT, NT])
        xn = sb("xn", [TT, 2, DIM])
        xt_a = sb("xt_a", [P, 2, TT])
        xt_b = sb("xt_b", [AUG, 2, TT])
        qx = sb("qx", [P, 2, MT, SH, TT])
        kt = sb("kt", [P, 2, MT, TT])
        vt = sb("vt", [TT, 2, HEADS, VW])
        mx = sb("mx", [TT, MT, P])
        pt = sb("pt", [TT, HEADS, TT])
        rs = sb("rs", [TT, HEADS])
        onorm = sb("onorm", [TT, DIM])
        xnt_a = sb("xnt_a", [P, NT * TT])
        xnt_b = sb("xnt_b", [AUG, NT * TT])
        logits = sb("logits", [TT, NT, EXPERTS])
        first = sb("first", [TT, NT, EXPERTS])
        second = sb("second", [TT, NT, EXPERTS])
        gm = sb("gm", [TT, 4, NT])
        gates = sb("gates", [TT, NT, EXPERTS])
        w1s = sb("w1s", [P, 2, 2, HID])
        w2s = sb("w2s", [P, 2, HC, DIM])
        ht = sb("ht", [P, 1, HC, BLK])
        res = h

        bank = [ctx.enter_context(nc.psum_tensor(f"bank{i}", [P, 512], f32)) for i in range(5)]
        s_ps = ctx.enter_context(nc.psum_tensor("s_ps", [P, 3, 512], f32))
        allbanks = [b[:, :] for b in bank] + [s_ps[:, i, :] for i in range(3)]
        v_ps, q_ps, k_ps, o_ps, m_ps = bank

        consts = sem("consts")
        wemb_in, wqkv_in, late_in = sem("wemb_in"), sem("wqkv_in"), sem("late_in")
        x_in = [sem("x_in0"), sem("x_in1")]
        zeroed, posb_a, posb_ready = sem("zeroed"), sem("posb_a"), sem("posb_ready")
        half_set = sem("half_set")
        em_done, ea_done = sem("em_done"), sem("ea_done")
        block = ctx.enter_context(nc.Block())

        L = [dict((n, sem(f"{n}_{l}")) for n in (
            "stat", "rstd", "xn", "t_done", "xt", "q_done", "k_done", "v_done", "q_ready", "k_ready",
            "v_ready", "s_done", "max", "mt_done", "m_ready", "st_done", "exp", "av", "rec", "nrm", "norm"))
            for l in range(2)]
        x0, xstat, xrstd = sem("x0"), sem("xstat"), sem("xrstd")
        ot_done, ot_ready, pj_done, x2, x2stat, x2rstd, resd = (
            sem(n) for n in ("ot_done", "ot_ready", "pj_done", "x2", "x2stat", "x2rstd", "resd"))
        nn, nt_done, nt_ready, g_done, logits_in, gchain, gdiff, gexp = (
            sem(n) for n in ("nn", "nt_done", "nt_ready", "g_done", "logits_in", "gchain", "gdiff", "gexp"))
        w_in = [sem("w_in0"), sem("w_in1")]
        h_done, gelu, y_done, y_added, stored = (sem(n) for n in ("h_done", "gelu", "y_done", "y_added", "stored"))

        CONSTS = 16 * (1 + 2 * TI + 4)

        @block.sync
        def _(sp):
            def load_group(g, p):
                sp.dma_start(patches[:, p].rearrange("p g c t -> p (g c t)"),
                             x[bass.ds(g, 1), :, :].rearrange("a p n -> (a p) n")).then_inc(x_in[p], 16)

            load_group(0, 0)
            sp.dma_start(ident[:, :], ident_in).then_inc(consts, 16)
            sp.dma_start(wemb[:, :, :], w_emb.rearrange("(c p) d -> p c d", p=P)).then_inc(wemb_in, 16)
            load_group(1, 1)
            for i in range(TI):
                sp.dma_start(posb[i * TOK:(i + 1) * TOK, :], pos).then_inc(consts, 16)
            sp.dma_start(bias_cls[:, :], tok_b).then_inc(posb_a, 16)
            sp.wait_ge(posb_a, 16)
            for i in range(TI):
                sp.dma_start(bias_cls[i * TOK:i * TOK + 1, :], cls).then_inc(consts, 16)
            for i in range(2):
                sp.dma_start(xt_b[D1:AUG, i, :], aug_in[:, 0:TT]).then_inc(consts, 16)
            sp.dma_start(xnt_b[D1:AUG, :], aug_in).then_inc(consts, 16)
            sp.dma_start(iota[:, :, :], iota_in).then_inc(consts, 16)
            sp.dma_start(wqka[:, :, :], wqk_a.rearrange("l p n -> p l n")).then_inc(wqkv_in, 16)
            sp.dma_start(wqkb[:, :, :], wqk_b.rearrange("l p n -> p l n")).then_inc(wqkv_in, 16)
            sp.dma_start(wva[:, :, :], wv_a.rearrange("l p n -> p l n")).then_inc(wqkv_in, 16)
            sp.dma_start(wvb[:, :, :], wv_b.rearrange("l p n -> p l n")).then_inc(wqkv_in, 16)
            sp.dma_start(lnw[:, 0, :], ln1).then_inc(late_in, 16)
            sp.dma_start(lnw[:, 1, :], ln2).then_inc(late_in, 16)
            sp.dma_start(projw[:, 0, :], proj[0:P, :]).then_inc(late_in, 16)
            sp.dma_start(projw[0:D1 + 1, 1, :], proj[P:, :]).then_inc(late_in, 16)
            sp.dma_start(gatew[:, 0, :], gate[0:P, :]).then_inc(late_in, 16)
            sp.dma_start(gatew[0:D1, 1, :], gate[P:, :]).then_inc(late_in, 16)
            with sp.Fori(2, NG - 1, 2) as g:
                for p in range(2):
                    sp.wait_ge(em_done, (g + p - 1) * GT)
                    load_group(g + p, p)
            sp.wait_ge(em_done, (NG - 2) * GT)
            load_group(NG - 1, 0)

            def load_expert(e, p):
                sp.dma_start(w1s[:, p, 0, :], w1[e, 0:P, :]).then_inc(w_in[p], 16)
                sp.dma_start(w1s[0:D1, p, 1, :], w1[e, P:, :]).then_inc(w_in[p], 16)
                sp.dma_start(w1s[D1:D1 + 1, p, 1, :], b1[bass.ds(e, 1), :]).then_inc(w_in[p], 16)
                sp.dma_start(b2s[D1:D1 + 1, p, :], b2[bass.ds(e, 1), :]).then_inc(w_in[p], 16)
                sp.dma_start(w2s[:, p, :, :], w2[e].rearrange("(c p) d -> p c d", p=P)).then_inc(w_in[p], 16)

            for e in range(2):
                load_expert(e, e)
            with sp.Fori(2, EXPERTS - 1, 2) as e:
                for p in range(2):
                    sp.wait_ge(y_done, (e + (p - 1)) * NB + 1)
                    load_expert(e + p, p)
            with sp.Fori(0, NT - 1) as t:
                sp.wait_ge(y_added, (EXPERTS - 1) * NT + t + 2)
                sp.dma_start(out[bass.ds(t, 1), :, :].rearrange("a t d -> (a t) d"),
                             res[:, bass.ds(t, 1), :].rearrange("p a d -> p (a d)")).then_inc(stored, 16)
            sp.wait_ge(y_added, EXPERTS * NT + 1)
            sp.dma_start(out[NT - 1, 0:TAIL, :], res[0:TAIL, NT - 1, :]).then_inc(stored, 16)
            sp.wait_ge(stored, 16 * NT)

        @block.tensor
        def _(pe):
            def embed(g, p):
                pe.wait_ge(x_in[p], 8 * (g - p) + 16)
                for j in range(GT):
                    if not isinstance(g, int) or g >= 1:
                        pe.wait_ge(ea_done, g * GT + j - 1)
                    for c in range(KC):
                        last = nc.tensor.matmul(allbanks[6 + j % 2][0:TT, 0:DIM],
                                                patches[:, p, j, c, :], wemb[:, c, :],
                                                start=(c == 0), stop=(c == KC - 1))
                    last.then_inc(em_done, 1)

            pe.wait_ge(consts, CONSTS)
            pe.wait_ge(wemb_in, 16)
            embed(0, 0)
            with pe.Fori(1, NG - 1, 2) as g:
                embed(g, 1)
                embed(g + 1, 0)

            pe.wait_ge(wqkv_in, 64)
            for l in range(2):
                s = L[l]

                def tr(t, p):
                    pe.wait_ge(s["xn"], t + 1)
                    if not isinstance(t, int) or t >= 1:
                        pe.wait_ge(s["xt"], t)
                    nc.tensor.transpose(o_ps[:, 256:256 + TT], xn[:, p, 0:P], ident[0:TT, 0:TT])
                    nc.tensor.transpose(o_ps[0:D1, 384:384 + TT], xn[:, p, P:DIM],
                                        ident[0:TT, 0:TT]).then_inc(s["t_done"], 1)

                def qkv(t, p):
                    pe.wait_ge(s["xt"], t + 1)
                    for o, ps, name in ((0, q_ps, "q_done"), (MT, k_ps, "k_done")):
                        for m in range(MT):
                            c0 = (o + m) * P
                            nc.tensor.matmul(ps[:, m * TT:(m + 1) * TT], wqka[:, l, c0:c0 + P], xt_a[:, p, :],
                                             start=True, stop=False)
                            last = nc.tensor.matmul(ps[:, m * TT:(m + 1) * TT], wqkb[:, l, c0:c0 + P],
                                                    xt_b[:, p, :], start=False, stop=True)
                        last.then_inc(s[name], 1)
                    if not isinstance(t, int) or t >= 1:
                        pe.wait_ge(s["v_ready"], t)
                    nc.tensor.matmul(v_ps[0:TT, 0:HEADS * VW], xt_a[:, p, :], wva[:, l, :], start=True, stop=False)
                    nc.tensor.matmul(v_ps[0:TT, 0:HEADS * VW], xt_b[:, p, :], wvb[:, l, :], start=False,
                                     stop=True).then_inc(s["v_done"], 1)

                def scores(t, p):
                    pe.wait_ge(s["q_ready"], t + 1)
                    pe.wait_ge(s["k_ready"], t + 1)
                    for m in range(MT):
                        if not isinstance(t, int) or t >= 1:
                            pe.wait_ge(s["exp"], 3 * t - 2 + m)
                        for i in range(SH):
                            last = nc.tensor.matmul(s_ps[0:TT, m, i * TT:(i + 1) * TT], qx[:, p, m, i, :],
                                                    kt[:, p, m, :], start=True, stop=True)
                        last.then_inc(s["s_done"], 1)

                def max_t(t):
                    pe.wait_ge(s["max"], t + 1)
                    for m in range(MT):
                        last = nc.tensor.transpose(m_ps[:, m * TT:(m + 1) * TT], mx[:, m, :], ident[0:TT, 0:TT])
                    last.then_inc(s["mt_done"], 1)

                def scores_t(t, p):
                    pe.wait_ge(s["m_ready"], t + 1)
                    for m in range(MT):
                        nc.tensor.matmul(s_ps[0:TT, m, 0:SH * TT], kt[:, p, m, :],
                                         qx[:, p, m, :, :].rearrange("p i t -> p (i t)"),
                                         start=True, stop=True).then_inc(s["st_done"], 1)

                def attend(t, p):
                    pe.wait_ge(s["exp"], 3 * t + 3)
                    pe.wait_ge(s["v_ready"], t + 1)
                    if not isinstance(t, int) or t >= 1:
                        pe.wait_ge(s["norm"], t)
                    for hd in range(HEADS):
                        last = nc.tensor.matmul(o_ps[0:TT, hd * VW:(hd + 1) * VW], pt[:, hd, :], vt[:, p, hd, :],
                                                start=True, stop=True)
                    last.then_inc(s["av"], 1)

                def step(t, p):
                    scores(t, p)
                    if inside(t, 1):
                        qkv(t + 1, 1 - p)
                    max_t(t)
                    if inside(t, -1):
                        attend(t - 1, 1 - p)
                    if inside(t, 2):
                        tr(t + 2, p)
                    scores_t(t, p)

                tr(0, 0)
                tr(1, 1)
                qkv(0, 0)
                step(0, 0)
                with pe.Fori(1, NT - 4, 2) as t:
                    step(t, 1)
                    step(t + 1, 0)
                for t in range(NT - 3, NT):
                    step(t, t % 2)
                attend(NT - 1, 1)

            pe.wait_ge(late_in, 16 * 6)

            def oproj(t, p):
                pe.wait_ge(ot_ready, t + 1)
                if not isinstance(t, int) or t >= 2:
                    pe.wait_ge(x2, t - 1)
                nc.tensor.matmul(bank[2 + p][0:TT, 0:DIM], xt_a[:, p, :], projw[:, 0, :], start=True, stop=False)
                nc.tensor.matmul(bank[2 + p][0:TT, 0:DIM], xt_b[0:D1 + 1, p, :], projw[0:D1 + 1, 1, :],
                                 start=False, stop=True).then_inc(pj_done, 1)

            def pair(first, second):
                def two(t):
                    first(t + 1, 1)
                    second(t, 0)
                    first(t + 2, 0)
                    second(t + 1, 1)

                first(0, 0)
                two(0)
                with pe.Fori(2, NT - 3, 2) as t:
                    two(t)
                first(NT - 1, 1)
                second(NT - 2, 0)
                second(NT - 1, 1)

            def oproj_t(t, p):
                pe.wait_ge(nn, t + 1)
                if not isinstance(t, int) or t >= 2:
                    pe.wait_ge(ot_ready, t - 1)
                nc.tensor.transpose(bank[p][:, 0:TT], xn[:, p, 0:P], ident[0:TT, 0:TT])
                nc.tensor.transpose(bank[p][0:D1, P:P + TT], xn[:, p, P:DIM], ident[0:TT, 0:TT]).then_inc(ot_done, 1)

            pair(oproj_t, oproj)

            def n_t(t, p):
                pe.wait_ge(nn, NT + t + 1)
                if not isinstance(t, int) or t >= 2:
                    pe.wait_ge(nt_ready, t - 1)
                nc.tensor.transpose(bank[p][:, 0:TT], xn[:, p, 0:P], ident[0:TT, 0:TT])
                nc.tensor.transpose(bank[p][0:D1, P:P + TT], xn[:, p, P:DIM], ident[0:TT, 0:TT]).then_inc(nt_done, 1)

            def n_g(t, p):
                pe.wait_ge(nt_ready, t + 1)
                if not isinstance(t, int) or t >= 2:
                    pe.wait_ge(logits_in, t - 1)
                nc.tensor.matmul(bank[2 + p][0:TT, 0:EXPERTS], xt_a[:, p, :], gatew[:, 0, :], start=True, stop=False)
                nc.tensor.matmul(bank[2 + p][0:TT, 0:EXPERTS], xt_b[0:D1, p, :], gatew[0:D1, 1, :],
                                 start=False, stop=True).then_inc(g_done, 1)

            pair(n_t, n_g)

            nc.tensor.transpose(bank[4][0:TT, 0:TT], ident[0:TT, 0:TT], ident[0:TT, 0:TT]).then_inc(y_done, 1)
            def ex_h(col, p, n):
                if not isinstance(n, int) or n >= 1:
                    pe.wait_ge(gelu, n + 1)
                for c in range(HC):
                    o = s_ps[:, c // 2, (c % 2) * BLK:(c % 2 + 1) * BLK]
                    nc.tensor.matmul(o, w1s[:, p, 0, c * P:(c + 1) * P], xnt_a[:, bass.ds(col, BLK)],
                                     start=True, stop=False)
                    last = nc.tensor.matmul(o, w1s[0:D1 + 1, p, 1, c * P:(c + 1) * P],
                                            xnt_b[0:D1 + 1, bass.ds(col, BLK)], start=False, stop=True)
                last.then_inc(h_done, 1)

            def ex_y(p, n):
                pe.wait_ge(gelu, n + 2)
                if not isinstance(n, int) or n >= 1:
                    pe.wait_ge(y_added, BT * n + 1)
                for j in range(BT):
                    for c in range(HC):
                        nc.tensor.matmul(bank[j][0:TT, 0:DIM], ht[:, 0, c, j * TT:(j + 1) * TT],
                                         w2s[:, p, c, :], start=(c == 0), stop=False)
                    last = nc.tensor.matmul(bank[j][0:TT, 0:DIM], xt_b[D1:D1 + 1, 0, :], b2s[D1:D1 + 1, p, :],
                                            start=False, stop=True)
                last.then_inc(y_done, 1)

            with pe.Fori(0, EXPERTS - 1, 2) as e:
                for p in range(2):
                    with pe.Fori(0, NB) as b:
                        n = pe.snap((e + p) * NB + b)
                        col = pe.snap(b * BLK)
                        pe.wait_ge(w_in[p], 40 * e + 80)
                        ex_h(col, p, n)
                        ex_y(p, n)

        @block.vector
        def _(dve):
            V = nc.vector

            def emb_add(t, j):
                dve.wait_ge(em_done, t + 1)
                V.tensor_tensor(h[:, bass.ds(t, 1), :].rearrange("p a d -> p (a d)"),
                                allbanks[6 + j][0:TT, 0:DIM], posb[:, :], ALU.add).then_inc(ea_done, 1)
                tile_stats(h, t, 0, ea_done, L[0]["stat"])

            def tile_stats(src, t, which, written, stat_s):
                dve.wait_ge(written, t + 1)
                dve.wait_ge(zeroed, 2)
                V.bn_stats(stats[:, which, bass.ds(t, 1)].rearrange("p a h c -> p (a h c)"),
                           src[:, bass.ds(t, 1), :].rearrange("p a d -> p (a d)")).then_inc(stat_s, 1)

            def normalise(src, t, p, which, done):
                V.tensor_scalar(xn[:, p, :], src[:, bass.ds(t, 1), :].rearrange("p a d -> p (a d)"),
                                mean[:, which, bass.ds(t, 1)],
                                rstd[:, which, bass.ds(t, 1)], ALU.subtract, ALU.mult).then_inc(done, 1)

            V.memset(qx[:, :, :, :, :], 0.0).then_inc(zeroed, 1)
            V.memset(mx[:, :, :], 0.0).then_inc(zeroed, 1)
            dve.wait_ge(zeroed, 2)
            dve.wait_ge(consts, CONSTS)
            V.tensor_tensor(posb[:, :], posb[:, :], bias_cls[:, :], ALU.add).then_inc(posb_ready, 1)
            dve.wait_ge(posb_ready, 1)
            with dve.Fori(0, NT - 1, 2) as t:
                emb_add(t, 0)
                emb_add(t + 1, 1)

            dve.wait_ge(late_in, 16 * 6)
            for l in range(2):
                s = L[l]
                src, which = (h, 0) if l == 0 else (xall, 2)
                if l == 1:
                    dve.wait_ge(xrstd, RSTD_OPS)
                    with dve.Fori(0, NT) as t:
                        V.tensor_scalar(xall[:, bass.ds(t, 1), :].rearrange("p a d -> p (a d)"),
                                        h[:, bass.ds(t, 1), :].rearrange("p a d -> p (a d)"),
                                        mean[:, 1, bass.ds(t, 1)],
                                        rstd[:, 1, bass.ds(t, 1)], ALU.subtract, ALU.mult).then_inc(x0, 1)
                        tile_stats(xall, t, 2, x0, s["stat"])

                def ln(t, p):
                    normalise(src, t, p, which, s["xn"])

                def xt_ev(t, p):
                    dve.wait_ge(s["t_done"], t + 1)
                    if l == 0:
                        V.tensor_copy(xt_a[:, p, :], o_ps[:, 256:256 + TT])
                        V.tensor_copy(xt_b[0:D1, p, :], o_ps[0:D1, 384:384 + TT]).then_inc(s["xt"], 1)
                    else:
                        V.tensor_scalar(xt_a[:, p, :], o_ps[:, 256:256 + TT], lnw[:, 0, 0:1], lnw[:, 0, 1:2],
                                        ALU.mult, ALU.add)
                        V.tensor_scalar(xt_b[0:D1, p, :], o_ps[0:D1, 384:384 + TT], lnw[0:D1, 0, 2:3],
                                        lnw[0:D1, 0, 3:4], ALU.mult, ALU.add).then_inc(s["xt"], 1)

                def k_ev(t, p):
                    dve.wait_ge(s["k_done"], t + 1)
                    V.tensor_copy(kt[:, p, :, :].rearrange("p m t -> p (m t)"),
                                  k_ps[:, 0:MT * TT]).then_inc(s["k_ready"], 1)

                def v_ev(t, p):
                    dve.wait_ge(s["v_done"], t + 1)
                    if not isinstance(t, int) or t >= 2:
                        dve.wait_ge(s["av"], t - 1)
                    V.tensor_copy(vt[:, p, :, :].rearrange("p h d -> p (h d)"),
                                  v_ps[0:TT, 0:HEADS * VW]).then_inc(s["v_ready"], 1)

                def maxes(t):
                    for m in range(MT):
                        dve.wait_ge(s["s_done"], 3 * t + m + 1)
                        last = V.tensor_reduce(
                            mx[:, m, :].rearrange("p (i c) -> p i c", c=SLOT)[:, :, 0:1],
                            s_ps[0:TT, m, 0:SH * TT].rearrange("p (i t) -> p i t", t=TT), AX, ALU.max, negate=True)
                    last.then_inc(s["max"], 1)

                def take(t):
                    dve.wait_ge(s["av"], t + 1)
                    o = o_ps[0:TT, 0:HEADS * VW].rearrange("p (h d) -> p h d", d=VW)
                    V.reciprocal(rs[:, :], o[:, :, HD:VW].rearrange("p h a -> p (h a)")).then_inc(s["rec"], 1)
                    dve.wait_ge(s["rec"], t + 1)
                    tile = (onorm[:, :] if l == 0 else
                            oall[:, bass.ds(t, 1), :].rearrange("p a d -> p (a d)"))
                    V.tensor_tensor(tile.rearrange("p (h d) -> p h d", d=HD), o[:, :, 0:HD],
                                    rs[:, :].rearrange("p (h a) -> p h a", a=1).to_broadcast([TT, HEADS, HD]),
                                    ALU.mult).then_inc(s["norm"], 1)
                    if l == 0:
                        dve.wait_ge(s["norm"], t + 1)
                        ht_ = h[:, bass.ds(t, 1), :].rearrange("p a d -> p (a d)")
                        V.tensor_tensor(ht_, ht_, onorm[:, :], ALU.add).then_inc(s["nrm"], 1)
                        tile_stats(h, t, 1, s["nrm"], xstat)

                def step(t, p):
                    maxes(t)
                    if inside(t, 1):
                        k_ev(t + 1, 1 - p)
                        v_ev(t + 1, 1 - p)
                    if inside(t, 2):
                        xt_ev(t + 2, p)
                    if inside(t, -1):
                        take(t - 1)
                    if inside(t, 3):
                        ln(t + 3, 1 - p)

                dve.wait_ge(s["rstd"], RSTD_OPS)
                ln(0, 0)
                ln(1, 1)
                xt_ev(0, 0)
                ln(2, 0)
                xt_ev(1, 1)
                k_ev(0, 0)
                v_ev(0, 0)
                step(0, 0)
                with dve.Fori(1, NT - 4, 2) as t:
                    step(t, 1)
                    step(t + 1, 0)
                for t in range(NT - 3, NT):
                    step(t, t % 2)
                take(NT - 1)

            def pair(zero, first, second):
                def two(t):
                    first(t + 1, 1)
                    zero(t + 2, 0)
                    second(t, 0)
                    first(t + 2, 0)
                    zero(t + 3, 1)
                    second(t + 1, 1)

                zero(0, 0)
                zero(1, 1)
                first(0, 0)
                two(0)
                with dve.Fori(2, NT - 3, 2) as t:
                    two(t)
                first(NT - 1, 1)
                second(NT - 2, 0)
                second(NT - 1, 1)

            dve.wait_ge(L[1]["norm"], NT)

            def o_cp(t, p):
                V.tensor_copy(xn[:, p, :], oall[:, bass.ds(t, 1), :].rearrange("p a d -> p (a d)")).then_inc(nn, 1)

            def o_ev(t, p):
                dve.wait_ge(ot_done, t + 1)
                if not isinstance(t, int) or t >= 2:
                    dve.wait_ge(pj_done, t - 1)
                V.tensor_copy(xt_a[:, p, :], bank[p][:, 0:TT])
                V.tensor_copy(xt_b[0:D1, p, :], bank[p][0:D1, P:P + TT]).then_inc(ot_ready, 1)

            def o_add(t, p):
                dve.wait_ge(pj_done, t + 1)
                xs = xall[:, bass.ds(t, 1), :].rearrange("p a d -> p (a d)")
                V.tensor_tensor(xs, bank[2 + p][0:TT, 0:DIM], xs, ALU.add).then_inc(x2, 1)
                tile_stats(xall, t, 3, x2, x2stat)
                hs = h[:, bass.ds(t, 1), :].rearrange("p a d -> p (a d)")
                V.tensor_tensor(hs, hs, xs, ALU.add).then_inc(resd, 1)

            pair(o_cp, o_ev, o_add)

            dve.wait_ge(x2rstd, RSTD_OPS)

            def n_ln(t, p):
                normalise(xall, t, p, 3, nn)

            def n_ev(t, p):
                dve.wait_ge(nt_done, t + 1)
                if not isinstance(t, int) or t >= 2:
                    dve.wait_ge(g_done, t - 1)
                V.tensor_scalar(xt_a[:, p, :], bank[p][:, 0:TT], lnw[:, 1, 0:1], lnw[:, 1, 1:2], ALU.mult, ALU.add)
                V.tensor_scalar(xt_b[0:D1, p, :], bank[p][0:D1, P:P + TT], lnw[0:D1, 1, 2:3], lnw[0:D1, 1, 3:4],
                                ALU.mult, ALU.add)
                V.tensor_scalar(xnt_a[:, bass.ds(t * TT, TT)], bank[p][:, 0:TT], lnw[:, 1, 0:1], lnw[:, 1, 1:2],
                                ALU.mult, ALU.add)
                V.tensor_scalar(xnt_b[0:D1, bass.ds(t * TT, TT)], bank[p][0:D1, P:P + TT], lnw[0:D1, 1, 2:3],
                                lnw[0:D1, 1, 3:4], ALU.mult, ALU.add).then_inc(nt_ready, 1)

            def n_gate(t, p):
                dve.wait_ge(g_done, t + 1)
                V.tensor_copy(logits[:, bass.ds(t, 1), :].rearrange("p a e -> p (a e)"),
                              bank[2 + p][0:TT, 0:EXPERTS]).then_inc(logits_in, 1)

            dve.wait_ge(resd, NT)
            pair(n_ln, n_ev, n_gate)

            chained = [0]

            def link(ins):
                ins.then_inc(gchain, 1)
                chained[0] += 1
                dve.wait_ge(gchain, chained[0])

            def wide(a):
                return a.rearrange("p (t a) -> p t a", a=1).to_broadcast([TT, NT, EXPERTS])

            def find(onehot, top_):
                link(V.tensor_reduce(top_, logits[:, :, :], AX, ALU.max))
                link(V.tensor_tensor(onehot, logits[:, :, :], wide(top_), ALU.is_equal))
                link(V.tensor_scalar(onehot, onehot, -float(EXPERTS), float(EXPERTS), ALU.mult, ALU.add))
                link(V.tensor_tensor(onehot, onehot, iota[:, :, :], ALU.add))
                link(V.tensor_reduce(gm[:, 3, :], onehot, AX, ALU.min))
                link(V.tensor_tensor(onehot, iota[:, :, :], wide(gm[:, 3, :]), ALU.is_equal))

            dve.wait_ge(logits_in, NT)
            find(first[:, :, :], gm[:, 0, :])
            link(V.tensor_scalar(second[:, :, :], first[:, :, :], -1.0, 1.0, ALU.mult, ALU.add))
            link(V.tensor_tensor(logits[:, :, :], logits[:, :, :], second[:, :, :], ALU.mult))
            link(V.tensor_scalar(second[:, :, :], first[:, :, :], -3.0e38, None, ALU.mult))
            link(V.tensor_tensor(logits[:, :, :], logits[:, :, :], second[:, :, :], ALU.add))
            find(second[:, :, :], gm[:, 1, :])
            V.tensor_tensor(gm[:, 1, :], gm[:, 1, :], gm[:, 0, :], ALU.subtract).then_inc(gdiff, 1)
            dve.wait_ge(gexp, 1)
            link(V.tensor_scalar(gm[:, 0, :], gm[:, 1, :], 1.0, None, ALU.add))
            link(V.reciprocal(gm[:, 0, :], gm[:, 0, :]))
            link(V.tensor_tensor(gm[:, 1, :], gm[:, 1, :], gm[:, 0, :], ALU.mult))
            link(V.tensor_tensor(first[:, :, :], first[:, :, :], wide(gm[:, 0, :]), ALU.mult))
            link(V.tensor_tensor(second[:, :, :], second[:, :, :], wide(gm[:, 1, :]), ALU.mult))
            V.memset(gm[:, 2, :], 0.0).then_inc(y_added, 1)
            link(V.tensor_tensor(gates[:, :, :], first[:, :, :], second[:, :, :], ALU.add))

            with dve.Fori(0, EXPERTS) as e:
                with dve.Fori(0, NB) as b:
                    dve.wait_ge(y_done, e * NB + b + 2)
                    for j in range(BT):
                        hs = h[:, bass.ds(b * BT + j, 1), :].rearrange("p a d -> p (a d)")
                        g1 = gates[:, bass.ds(b * BT + j, 1), bass.ds(e, 1)].rearrange("p a e -> p (a e)")
                        V.scalar_tensor_tensor(out=hs, in0=bank[j][0:TT, 0:DIM], scalar=g1, in1=hs,
                                               op0=ALU.mult, op1=ALU.add).then_inc(y_added, 1)

        @block.scalar
        def _(act):
            A = nc.scalar

            act.wait_ge(zeroed, 2)
            for l in range(2):
                s = L[l]

                def q_ev(t, p):
                    act.wait_ge(s["q_done"], t + 1)
                    for i in range(SH):
                        last = A.copy(qx[i * SLOT:(i + 1) * SLOT, p, :, i, :],
                                      q_ps[i * SLOT:(i + 1) * SLOT, 0:MT * TT].rearrange("p (m t) -> p m t", t=TT))
                    last.then_inc(s["q_ready"], 1)

                def m_ev(t, p):
                    act.wait_ge(s["mt_done"], t + 1)
                    for i in range(SH):
                        last = A.copy(qx[i * SLOT:i * SLOT + 1, p, :, i, :],
                                      m_ps[i * SLOT:i * SLOT + 1, 0:MT * TT].rearrange("p (m t) -> p m t", t=TT))
                    last.then_inc(s["m_ready"], 1)

                def exps(t):
                    for m in range(MT):
                        act.wait_ge(s["st_done"], 3 * t + m + 1)
                        A.activation(pt[:, m * SH:(m + 1) * SH, :].rearrange("p h t -> p (h t)"),
                                     s_ps[0:TT, m, 0:SH * TT], ACT.Exp, scale=HD ** -0.5).then_inc(s["exp"], 1)

                def step(t, p):
                    if inside(t, 1):
                        q_ev(t + 1, 1 - p)
                    m_ev(t, p)
                    exps(t)

                q_ev(0, 0)
                step(0, 0)
                with act.Fori(1, NT - 4, 2) as t:
                    step(t, 1)
                    step(t + 1, 0)
                for t in range(NT - 3, NT):
                    step(t, t % 2)

            act.wait_ge(gdiff, 1)
            A.activation(gm[:, 1, :], gm[:, 1, :], ACT.Exp).then_inc(gexp, 1)
            A.copy(gap[:, 0:1], ident[0:TT, 0:1]).then_inc(gelu, 1)

            with act.Fori(0, EXPERTS * NB) as n:
                act.wait_ge(h_done, n + 1)
                act.wait_ge(y_done, n + 1)
                A.activation(ht[:, 0, :, :].rearrange("p (a c) t -> p a c t", c=2),
                             s_ps[:, :, 0:2 * BLK].rearrange("p a (c t) -> p a c t", c=2),
                             ACT.Gelu).then_inc(gelu, 1)

        @block.gpsimd
        def _(pool):
            pool.memset(half[:, :], -0.5).then_inc(half_set, 1)
            pool.wait_ge(half_set, 1)
            for which, stat_s, done in ((0, L[0]["stat"], L[0]["rstd"]), (1, xstat, xrstd),
                                        (2, L[1]["stat"], L[1]["rstd"]), (3, x2stat, x2rstd)):
                pool.wait_ge(stat_s, NT)

                def col(h_, c):
                    return stats[:, which, :, h_, c:c + 1].rearrange("p t a -> p (t a)")

                var = rstd[:, which, :]
                steps = (
                    lambda: pool.tensor_tensor(mean[:, which, :], col(0, 1), col(1, 1), ALU.add),
                    lambda: pool.tensor_scalar(mean[:, which, :], mean[:, which, :], 0.5, None, ALU.mult),
                    lambda: pool.tensor_tensor(gap[:, :], col(0, 1), mean[:, which, :], ALU.subtract),
                    lambda: pool.tensor_tensor(gap[:, :], gap[:, :], gap[:, :], ALU.mult),
                    lambda: pool.tensor_tensor(var, col(0, 2), col(1, 2), ALU.add),
                    lambda: pool.tensor_scalar(var, var, 1.0 / DIM, EPS, ALU.mult, ALU.add),
                    lambda: pool.tensor_tensor(var, var, gap[:, :], ALU.add),
                    lambda: pool.tensor_tensor(var, var, half[:, :], ALU.pow),
                )
                for n, op in enumerate(steps):
                    op().then_inc(done, 1)
                    if n + 1 < len(steps):
                        pool.wait_ge(done, n + 1)


def _slots(wa, ba, wb, bb):
    w = np.zeros((DIM + 4, 2, MT, SH, SLOT), np.float32)
    for n, (wm, bm) in enumerate(((wa, ba), (wb, bb))):
        w[:DIM, n, :, :, 4:4 + HD] = wm.reshape(DIM, MT, SH, HD)
        w[DIM, n, :, :, 4:4 + HD] = bm.reshape(MT, SH, HD)
    w[DIM, 1, :, :, 0] = 1.0
    for i in range(TI):
        w[DIM + 1 + i, 0, :, :, 1 + i] = 1.0
        w[DIM, 1, :, :, 1 + i] = -BIG
        w[DIM + 1 + i, 1, :, :, 1 + i] = BIG
    return w.reshape(DIM + 4, 2 * MT * P)


def _values(wm, bm):
    w = np.zeros((DIM + 4, HEADS, VW), np.float32)
    w[:DIM, :, :HD] = wm.reshape(DIM, HEADS, HD)
    w[DIM, :, :HD] = bm.reshape(HEADS, HD)
    w[DIM, :, HD] = 1.0
    return w.reshape(DIM + 4, HEADS * VW)


def kernel(**inputs):
    import concourse.bacc as bacc
    from concourse.bass_utils import run_bass_kernel_spmd

    a = {k: np.asarray(v) for k, v in inputs.items()}
    qkv_w = a["L0_ffn_qkv_w"].reshape(DIM, 3, DIM)
    qkv_b = a["L0_ffn_qkv_b"].reshape(3, DIM)
    qk = np.stack([_slots(a["L0_attn_Wq"].T, a["L0_attn_bq"], a["L0_attn_Wk"].T, a["L0_attn_bk"]),
                   _slots(qkv_w[:, 0], qkv_b[0], qkv_w[:, 1], qkv_b[1])])
    vv = np.stack([_values(a["L0_attn_Wv"].T, a["L0_attn_bv"]), _values(qkv_w[:, 2], qkv_b[2])])

    def ln(g, b):
        w = np.zeros((P, 4), np.float32)
        w[:, 0], w[:, 1] = g[:P], b[:P]
        w[:D1, 2], w[:D1, 3] = g[P:], b[P:]
        return w

    aug = np.zeros((4, NT * TT), np.float32)
    aug[0] = 1.0
    for i in range(TI):
        aug[1 + i] = np.tile(np.repeat(np.arange(TI) == i, TOK), NT)
    pt = a["x"].reshape(IMAGES, CHANNELS, PER_SIDE, PATCH, PER_SIDE, PATCH).transpose(0, 1, 2, 4, 3, 5)
    px = np.zeros((NT * TI, TOK, PIX), np.float32)
    px[:IMAGES, 1:] = pt.reshape(IMAGES, PATCHES, PIX)
    px = px.reshape(NG, GT, TT, KC, P).transpose(0, 4, 1, 3, 2).reshape(NG, P, GT * KC * TT)
    arrays = {
        "x": px, "pos": a["L0_tok_pos_embedding"],
        "tok_b": np.repeat(a["L0_tok_b"].reshape(1, DIM), TT, 0), "cls": a["L0_tok_class_token"],
        "w_emb": a["L0_tok_W"].T,
        "wqk_a": qk[:, :P], "wqk_b": qk[:, P:], "wv_a": vv[:, :P], "wv_b": vv[:, P:],
        "ln1": ln(a["L0_ffn_ln1_g"], a["L0_ffn_ln1_b"]), "ln2": ln(a["L0_ffn_ln2_g"], a["L0_ffn_ln2_b"]),
        "proj": np.concatenate([a["L0_ffn_proj_w"], a["L0_ffn_proj_b"].reshape(1, DIM)]),
        "gate": a["L0_ffn_gate_w"], "w1": a["L0_ffn_w1"], "b1": a["L0_ffn_b1"],
        "w2": a["L0_ffn_w2"], "b2": a["L0_ffn_b2"],
        "ident": np.eye(P, dtype=np.float32), "aug": aug,
        "iota": np.tile(np.arange(EXPERTS, dtype=np.float32), (TT, NT, 1)),
    }
    arrays = {k: np.ascontiguousarray(v) for k, v in arrays.items()}
    nc = bacc.Bacc("TRN2", target_bir_lowering=False, num_devices=1)
    args = [nc.dram_tensor(f"in_{k}", v.shape, mybir.dt.from_np(v.dtype), kind="ExternalInput").ap()
            for k, v in arrays.items()]
    out = nc.dram_tensor("out", (NT, TT, DIM), mybir.dt.float32, kind="ExternalOutput").ap()
    build(nc, *args, out)
    r = run_bass_kernel_spmd(nc, [{f"in_{k}": v for k, v in arrays.items()}], core_ids=[0])
    return r.results[0]["out"].reshape(NT * TT, DIM)[:IMAGES * TOK].reshape(IMAGES, TOK, DIM)
```

```python
import numpy as np
import concourse.bass as bass
from concourse import mybir
from contextlib import ExitStack

IMAGES, CHANNELS, SIDE, PATCH = 64, 3, 96, 16
PER_SIDE = SIDE // PATCH
PATCHES = PER_SIDE * PER_SIDE
TOK = PATCHES + 1
DIM, HEADS = 192, 12
HD = DIM // HEADS
EXPERTS, HID = 8, 768
PIX = CHANNELS * PATCH * PATCH
P = 128
TI = 3
TT = TI * TOK
NT = -(-IMAGES // TI)
TAIL = (IMAGES - (NT - 1) * TI) * TOK
GT = 2
NG = NT // GT
KC = PIX // P
D1 = DIM - P
AUG = D1 + 4
SLOT = 32
SH = P // SLOT
MT = HEADS // SH
VW = HD + 1
BIG = float(2 ** 40)
EPS = 1e-5
RSTD_OPS = 8
HC = HID // P
SUB = 2
ST = SUB * P
NS = (2 * IMAGES * TOK + EXPERTS * (ST - 1)) // ST
NSLOT = NS * ST
XW = DIM + 2
OUTSIDE = 8192
MAXT = -(-IMAGES * TOK // ST)
XS, W1S, W2S = 16.0, 256.0, 256.0
AHEAD = 4
PREP = 9
CHUNKS = ((0, 6, TT), (6, 6, TT), (12, 5, TT), (17, NT - 18, TT), (NT - 1, 1, TAIL))


def inside(t, off):
    return not isinstance(t, int) or 0 <= t + off < NT


def build(nc, x, pos, tok_b, cls, w_emb, wqk_a, wqk_b, wv_a, wv_b, ln1, ln2_g, ln2_b, proj, gate, w1, b1, w2, b2,
          ident_in, aug_in, route_in, tri_in, neg_in, slots, ymoe, out):
    f32 = mybir.dt.float32
    i32, f16 = mybir.dt.int32, mybir.dt.float16
    ALU, ACT, AX = mybir.AluOpType, mybir.ActivationFunctionType, mybir.AxisListType.X
    ctx = ExitStack()
    with ctx:
        def sb(name, shape, dt=f32):
            return ctx.enter_context(nc.sbuf_tensor(name, shape, dt))

        def sem(name):
            return ctx.enter_context(nc.semaphore(name))

        ident = sb("ident", [P, P])
        posbuf = sb("posbuf", [TT, 2 * DIM])
        posb, bias_cls = posbuf[:, 0:DIM], posbuf[:, DIM:2 * DIM]
        wqka = sb("wqka", [P, 2, 2 * MT * P])
        wqkb = sb("wqkb", [P, 2, 2 * MT * P])
        wva = sb("wva", [P, 2, HEADS * VW])
        wvb = sb("wvb", [AUG, 2, HEADS * VW])
        lnw = sb("lnw", [P, 4])
        ln2w = sb("ln2w", [TT, 2, DIM])
        projw = sb("projw", [P, 2, DIM])
        gatew = sb("gatew", [P, 2, EXPERTS])
        neg = sb("neg", [P, 2])
        embbuf = sb("embbuf", [P, 2 * GT * KC * TT + KC * DIM])
        patches = embbuf[:, 0:2 * GT * KC * TT].rearrange("p (b g c t) -> p b g c t", b=2, g=GT, c=KC)
        wemb = embbuf[:, 2 * GT * KC * TT:].rearrange("p (c d) -> p c d", d=DIM)
        st_a, st_b, st_l = (embbuf[:, i * HID:(i + 1) * HID] for i in range(3))
        st_w2 = embbuf[:, 3 * HID:3 * HID + HC * DIM]
        st_b2 = embbuf[0:2, 3 * HID + HC * DIM:3 * HID + HC * DIM + DIM]
        tmp_l = sb("tmp_l", [D1 + 2, HID], f16)
        tmp_b2 = sb("tmp_b2", [2, DIM], f16)
        w1ah = sb("w1ah", [P, EXPERTS * HID], f16)
        w1al = sb("w1al", [P, EXPERTS * HID], f16)
        w1bh = sb("w1bh", [P, EXPERTS * HID], f16)
        w1bl = sb("w1bl", [D1 + 2, EXPERTS * HID], f16)
        w2h = sb("w2h", [P, EXPERTS * HC * DIM], f16)
        w2l = sb("w2l", [P, EXPERTS * HC * DIM], f16)
        b2hl = sb("b2hl", [2, EXPERTS * DIM], f16)
        h = sb("h", [TT, NT, DIM])
        rows0 = sb("rows0", [TT, NT, XW])
        rows1 = sb("rows1", [TT, NT, XW])
        xall, oall = rows0[:, :, 0:DIM], rows1[:, :, 0:DIM]
        rows16 = rows0[:, :, 0:DIM].bitcast(f16)
        stats = sb("stats", [TT, 4, NT, 2, 3])
        mean = sb("mean", [TT, 4, NT])
        rstd = sb("rstd", [TT, 4, NT])
        gap = sb("gap", [TT, NT])
        half = sb("half", [TT, NT])
        xn = sb("xn", [TT, 2, DIM])
        xt_a = sb("xt_a", [P, 2, TT])
        xt_b = sb("xt_b", [AUG, 2, TT])
        qxbuf = sb("qxbuf", [P, 2 * MT * SH * TT])
        qx = qxbuf[:, :].rearrange("p (b m i t) -> p b m i t", b=2, m=MT, i=SH)
        ktbuf = sb("ktbuf", [P, 2 * MT * TT])
        kt = ktbuf[:, :].rearrange("p (b m t) -> p b m t", b=2, m=MT)
        vt = sb("vt", [TT, 2, HEADS, VW])
        mx = sb("mx", [TT, MT, P])
        ptbuf = sb("ptbuf", [P, HEADS * TT])
        pt = ptbuf[0:TT, :].rearrange("p (h t) -> p h t", t=TT)
        rs = sb("rs", [TT, HEADS])
        onorm = sb("onorm", [TT, DIM])
        spare = wqka[:, :, :].rearrange("p l n -> p (l n)")
        NE = NT * EXPERTS
        first, second, oh, cnt, place, logits = (
            spare[0:TT, i * NE:(i + 1) * NE].rearrange("p (t e) -> p t e", e=EXPERTS) for i in range(6))
        etf = wva[0:1, :, :].rearrange("p l n -> p (l n)")[:, 0:NS * EXPERTS].rearrange(
            "p (s e) -> p s e", e=EXPERTS)
        gm = sb("gm", [TT, 4, NT])
        pos_i = sb("pos_i", [TT, 2, NT], i32)
        small = sb("small", [TT, 4, EXPERTS])
        etab = sb("etab", [1, NS], i32)
        etn = sb("etn", [1, NS])
        RC = {}
        at = 0
        for name, shape in (("iota", (NT, EXPERTS)), ("thr", (EXPERTS, MAXT)), ("tri8", (EXPERTS, EXPERTS)),
                            ("tile", (NS, EXPERTS)), ("dest", (2, NT)), ("outside", (1, NT)), ("valid", (1, NT)),
                            ("ones", (1, NT))):
            RC[name] = (at, shape)
            at += shape[0] * shape[1]
        route = sb("route", [TT, at])

        def rc(name, rows=TT):
            o, (a, b) = RC[name]
            return route[0:rows, o:o + a * b].rearrange("p (a b) -> p a b", b=b)

        tri = posbuf[:, 0:2 * TT].rearrange("p (a t) -> p a t", a=2)
        h32 = qxbuf[:, 0:HC * ST]
        hh = [qxbuf[:, HC * ST:HC * ST * 3 // 2].bitcast(f16), ptbuf[:, 0:HC * ST // 2].bitcast(f16)]
        hl = [wqkb[:, :, :].rearrange("p l n -> p (l n)")[:, i * HC * ST // 2:(i + 1) * HC * ST // 2].bitcast(f16)
              for i in range(2)]
        xs = [v.rearrange("p (j n) -> p j n", j=SUB)
              for v in (ptbuf[:, HC * ST // 2:HC * ST // 2 + SUB * XW], ktbuf[:, 0:SUB * XW])]
        yg = spare[:, 0:2 * SUB * DIM].rearrange("p (b j d) -> p b j d", b=2, j=SUB)
        xt16 = spare[:, 2 * SUB * DIM:4 * SUB * DIM].bitcast(f16).rearrange("p (b i n) -> p b i n", b=2, i=3)
        xl16 = sb("xl16", [D1 + 2, 2, ST], f16)
        ones16 = sb("ones16", [2, P], f16)
        identh = sb("identh", [P, P], f16)
        dest = sb("dest", [P, 2, SUB], i32)
        fields = sb("fields", [P, NS, SUB, 2])

        psum = ctx.enter_context(nc.psum_tensor("psum", [P, 8, 512], f32))
        bank = [psum[:, i, :] for i in range(5)]
        s_ps = psum[:, 5:8, :]
        allbanks = [psum[:, i, :] for i in range(8)]
        v_ps, q_ps, k_ps, o_ps, m_ps = bank

        consts = sem("consts")
        wemb_in, wqkv_in, late_in = sem("wemb_in"), sem("wqkv_in"), sem("late_in")
        x_in = [sem("x_in0"), sem("x_in1")]
        zeroed, posb_a, posb_ready = sem("zeroed"), sem("posb_a"), sem("posb_ready")
        half_set = sem("half_set")
        em_done, ea_done = sem("em_done"), sem("ea_done")
        block = ctx.enter_context(nc.Block())

        L = [dict((n, sem(f"{n}_{l}")) for n in (
            "stat", "rstd", "xn", "t_done", "xt", "q_done", "k_done", "v_done", "q_ready", "k_ready",
            "v_ready", "s_done", "max", "mt_done", "m_ready", "st_done", "exp", "av", "rec", "nrm", "norm"))
            for l in range(2)]
        x0, xstat, xrstd = sem("x0"), sem("xstat"), sem("xrstd")
        ot_done, ot_ready, pj_done, x2, x2stat, x2rstd, resd = (
            sem(n) for n in ("ot_done", "ot_ready", "pj_done", "x2", "x2stat", "x2rstd", "resd"))
        nn, nt_done, nt_ready, g_done, logits_in, gchain, gdiff, gexp = (
            sem(n) for n in ("nn", "nt_done", "nt_ready", "g_done", "logits_in", "gchain", "gdiff", "gexp"))
        w_in, w_scaled, w_high, w_low = sem("w_in"), sem("w_scaled"), sem("w_high"), sem("w_low")
        ln2_scaled, yn, ync, row_split, row_copied = (
            sem(n) for n in ("ln2_scaled", "yn", "ync", "row_split", "row_copied"))
        tri_loaded = sem("tri_loaded")
        row_high = sem("row_high")
        oh_ready, ranked, routed, cleared, scattered, small_set = (
            sem(n) for n in ("oh_ready", "ranked", "routed", "cleared", "scattered", "small_set"))
        xs_in = [sem("xs_in0"), sem("xs_in1")]
        y_out = [sem("y_out0"), sem("y_out1")]
        tt_done, xe, h_done, gelu, hi_done, split, y_done, y_ev, fields_in = (
            sem(n) for n in ("tt_done", "xe", "h_done", "gelu", "hi_done", "split", "y_done", "y_ev", "fields_in"))
        back = [sem(f"back{i}") for i in range(len(CHUNKS))]
        summed, added, stored = sem("summed"), sem("added"), sem("stored")

        CONSTS = 16 * (1 + 2 * TI + 2 + 2)

        @block.sync
        def _(sp):
            def load_group(g, p):
                sp.dma_start(patches[:, p].rearrange("p g c t -> p (g c t)"),
                             x[bass.ds(g, 1), :, :].rearrange("a p n -> (a p) n")).then_inc(x_in[p], 16)

            load_group(0, 0)
            sp.dma_start(ident[:, :], ident_in).then_inc(consts, 16)
            sp.dma_start(wemb[:, :, :], w_emb.rearrange("(c p) d -> p c d", p=P)).then_inc(wemb_in, 16)
            load_group(1, 1)
            for i in range(TI):
                sp.dma_start(posb[i * TOK:(i + 1) * TOK, :], pos).then_inc(consts, 16)
            sp.dma_start(bias_cls, tok_b).then_inc(posb_a, 16)
            sp.wait_ge(posb_a, 16)
            for i in range(TI):
                sp.dma_start(bias_cls[i * TOK:i * TOK + 1, :], cls).then_inc(consts, 16)
            for i in range(2):
                sp.dma_start(xt_b[D1:AUG, i, :], aug_in[:, 0:TT]).then_inc(consts, 16)
            sp.dma_start(route[:, :], route_in).then_inc(consts, 16)
            sp.dma_start(neg[:, :], neg_in).then_inc(consts, 16)
            sp.dma_start(wqka[:, :, :], wqk_a.rearrange("l p n -> p l n")).then_inc(wqkv_in, 16)
            sp.dma_start(wqkb[0:AUG, :, :], wqk_b.rearrange("l p n -> p l n")).then_inc(wqkv_in, 16)
            sp.dma_start(wva[:, :, :], wv_a.rearrange("l p n -> p l n")).then_inc(wqkv_in, 16)
            sp.dma_start(wvb[:, :, :], wv_b.rearrange("l p n -> p l n")).then_inc(wqkv_in, 16)
            sp.dma_start(lnw[:, :], ln1).then_inc(late_in, 16)
            sp.dma_start(ln2w[:, 0, :], ln2_g).then_inc(late_in, 16)
            sp.dma_start(ln2w[:, 1, :], ln2_b).then_inc(late_in, 16)
            sp.dma_start(projw[:, 0, :], proj[0:P, :]).then_inc(late_in, 16)
            sp.dma_start(projw[0:D1 + 1, 1, :], proj[P:, :]).then_inc(late_in, 16)
            sp.dma_start(gatew[:, 0, :], gate[0:P, :]).then_inc(late_in, 16)
            sp.dma_start(gatew[0:D1, 1, :], gate[P:, :]).then_inc(late_in, 16)
            with sp.Fori(2, NG - 1, 2) as g:
                for p in range(2):
                    sp.wait_ge(em_done, (g + p - 1) * GT)
                    load_group(g + p, p)
            sp.wait_ge(em_done, (NG - 2) * GT)
            load_group(NG - 1, 0)

            sp.wait_ge(zeroed, 3)
            sp.dma_start(slots.rearrange("(s p) n -> p s n", p=P),
                         w1ah[:, 0:2 * XW].bitcast(f32).rearrange("p (a n) -> p a n", a=1).to_broadcast([P, SUB * NS, XW])).then_inc(cleared, 16)

            def load_expert(e):
                for dst, src in ((st_a, w1[bass.ds(e, 1), 0:P, :]), (st_b[0:D1], w1[bass.ds(e, 1), P:, :]),
                                 (st_b[D1:P], w1[bass.ds(e, 1), P:, :]), (st_l[0:D1], w1[bass.ds(e, 1), P:, :])):
                    sp.dma_start(dst, src.rearrange("a p n -> (a p) n")).then_inc(w_in, 16)
                for i in range(2):
                    sp.dma_start(st_l[D1 + i:D1 + i + 1], b1[bass.ds(e, 1), :]).then_inc(w_in, 16)
                    sp.dma_start(st_b2[i:i + 1], b2[bass.ds(e, 1), :]).then_inc(w_in, 16)
                sp.dma_start(st_w2.rearrange("p (c d) -> p c d", d=DIM),
                             w2[bass.ds(e, 1)].rearrange("a (c p) d -> p (a c) d", p=P)).then_inc(w_in, 16)

            sp.wait_ge(em_done, NT)
            sp.wait_ge(ea_done, NT)
            sp.dma_start(tri, tri_in).then_inc(tri_loaded, 16)
            load_expert(0)
            with sp.Fori(1, EXPERTS) as e:
                sp.wait_ge(w_low, e)
                load_expert(e)

            def load_slots(s_, p):
                sp.dma_start(xs[p], slots[bass.ds(s_ * ST, ST), :].rearrange("(j p) n -> p j n", p=P)).then_inc(xs_in[p], 16)

            sp.wait_ge(scattered, 16 * 2 * NT)
            load_slots(0, 0)
            load_slots(1, 1)
            with sp.Fori(2, NS - 1, 2) as s_:
                for p in range(2):
                    sp.wait_ge(tt_done, s_ + (p - 1))
                    sp.wait_ge(fields_in, s_ + (p - 1))
                    load_slots(s_ + p, p)

            for p in range(2):
                sp.wait_ge(y_out[p], 16 * SUB * NS // 2)
            for n, (t0, k, r) in enumerate(CHUNKS):
                for i, dst in enumerate((xall, oall)):
                    sp.dma_start(dst[0:r, t0:t0 + k, :],
                                 ymoe[(i * NT + t0) * TT:(i * NT + t0) * TT + (k - 1) * TT + r, :].rearrange(
                                     "(t p) d -> p t d", p=r)).then_inc(back[n], 16)
            for n, (t0, k, r) in enumerate(CHUNKS):
                sp.wait_ge(added, n + 1)
                sp.dma_start(out[t0:t0 + k, 0:r, :].rearrange("t p d -> p t d"), h[0:r, t0:t0 + k, :]).then_inc(stored, 16)
            sp.wait_ge(stored, 16 * len(CHUNKS))

        @block.tensor
        def _(pe):
            def embed(g, p):
                pe.wait_ge(x_in[p], 8 * (g - p) + 16)
                for j in range(GT):
                    if not isinstance(g, int) or g >= 1:
                        pe.wait_ge(ea_done, g * GT + j - 1)
                    for c in range(KC):
                        last = nc.tensor.matmul(allbanks[6 + j % 2][0:TT, 0:DIM],
                                                patches[:, p, j, c, :], wemb[:, c, :],
                                                start=(c == 0), stop=(c == KC - 1))
                    last.then_inc(em_done, 1)

            pe.wait_ge(consts, CONSTS)
            pe.wait_ge(wemb_in, 16)
            embed(0, 0)
            with pe.Fori(1, NG - 1, 2) as g:
                embed(g, 1)
                embed(g + 1, 0)

            pe.wait_ge(wqkv_in, 64)
            for l in range(2):
                s = L[l]

                def tr(t, p):
                    pe.wait_ge(s["xn"], t + 1)
                    if not isinstance(t, int) or t >= 1:
                        pe.wait_ge(s["xt"], t)
                    nc.tensor.transpose(o_ps[:, 256:256 + TT], xn[:, p, 0:P], ident[0:TT, 0:TT])
                    nc.tensor.transpose(o_ps[0:D1, 384:384 + TT], xn[:, p, P:DIM],
                                        ident[0:TT, 0:TT]).then_inc(s["t_done"], 1)

                def qkv(t, p):
                    pe.wait_ge(s["xt"], t + 1)
                    for o, ps, name in ((0, q_ps, "q_done"), (MT, k_ps, "k_done")):
                        for m in range(MT):
                            c0 = (o + m) * P
                            nc.tensor.matmul(ps[:, m * TT:(m + 1) * TT], wqka[:, l, c0:c0 + P], xt_a[:, p, :],
                                             start=True, stop=False)
                            last = nc.tensor.matmul(ps[:, m * TT:(m + 1) * TT], wqkb[0:AUG, l, c0:c0 + P],
                                                    xt_b[:, p, :], start=False, stop=True)
                        last.then_inc(s[name], 1)
                    if not isinstance(t, int) or t >= 1:
                        pe.wait_ge(s["v_ready"], t)
                    nc.tensor.matmul(v_ps[0:TT, 0:HEADS * VW], xt_a[:, p, :], wva[:, l, :], start=True, stop=False)
                    nc.tensor.matmul(v_ps[0:TT, 0:HEADS * VW], xt_b[:, p, :], wvb[:, l, :], start=False,
                                     stop=True).then_inc(s["v_done"], 1)

                def scores(t, p):
                    pe.wait_ge(s["q_ready"], t + 1)
                    pe.wait_ge(s["k_ready"], t + 1)
                    for m in range(MT):
                        if not isinstance(t, int) or t >= 1:
                            pe.wait_ge(s["exp"], 3 * t - 2 + m)
                        for i in range(SH):
                            last = nc.tensor.matmul(s_ps[0:TT, m, i * TT:(i + 1) * TT], qx[:, p, m, i, :],
                                                    kt[:, p, m, :], start=True, stop=True)
                        last.then_inc(s["s_done"], 1)

                def max_t(t):
                    pe.wait_ge(s["max"], t + 1)
                    for m in range(MT):
                        last = nc.tensor.transpose(m_ps[:, m * TT:(m + 1) * TT], mx[:, m, :], ident[0:TT, 0:TT])
                    last.then_inc(s["mt_done"], 1)

                def scores_t(t, p):
                    pe.wait_ge(s["m_ready"], t + 1)
                    for m in range(MT):
                        nc.tensor.matmul(s_ps[0:TT, m, 0:SH * TT], kt[:, p, m, :],
                                         qx[:, p, m, :, :].rearrange("p i t -> p (i t)"),
                                         start=True, stop=True).then_inc(s["st_done"], 1)

                def attend(t, p):
                    pe.wait_ge(s["exp"], 3 * t + 3)
                    pe.wait_ge(s["v_ready"], t + 1)
                    if not isinstance(t, int) or t >= 1:
                        pe.wait_ge(s["norm"], t)
                    for hd in range(HEADS):
                        last = nc.tensor.matmul(o_ps[0:TT, hd * VW:(hd + 1) * VW], pt[:, hd, :], vt[:, p, hd, :],
                                                start=True, stop=True)
                    last.then_inc(s["av"], 1)

                def step(t, p):
                    scores(t, p)
                    if inside(t, 1):
                        qkv(t + 1, 1 - p)
                    max_t(t)
                    if inside(t, -1):
                        attend(t - 1, 1 - p)
                    if inside(t, 2):
                        tr(t + 2, p)
                    scores_t(t, p)

                tr(0, 0)
                tr(1, 1)
                qkv(0, 0)
                step(0, 0)
                with pe.Fori(0, EXPERTS) as e:
                    step(2 * e + 1, 1)
                    step(2 * e + 2, 0)
                for t in range(2 * EXPERTS + 1, NT):
                    step(t, t % 2)
                attend(NT - 1, 1)

            pe.wait_ge(late_in, 16 * 7)

            def oproj(t, p):
                pe.wait_ge(ot_ready, t + 1)
                if not isinstance(t, int) or t >= 2:
                    pe.wait_ge(x2, t - 1)
                nc.tensor.matmul(bank[2 + p][0:TT, 0:DIM], xt_a[:, p, :], projw[:, 0, :], start=True, stop=False)
                nc.tensor.matmul(bank[2 + p][0:TT, 0:DIM], xt_b[0:D1 + 1, p, :], projw[0:D1 + 1, 1, :],
                                 start=False, stop=True).then_inc(pj_done, 1)

            def pair(first, second):
                def two(t):
                    first(t + 1, 1)
                    second(t, 0)
                    first(t + 2, 0)
                    second(t + 1, 1)

                first(0, 0)
                two(0)
                with pe.Fori(2, NT - 3, 2) as t:
                    two(t)
                first(NT - 1, 1)
                second(NT - 2, 0)
                second(NT - 1, 1)

            def oproj_t(t, p):
                pe.wait_ge(nn, t + 1)
                if not isinstance(t, int) or t >= 2:
                    pe.wait_ge(ot_ready, t - 1)
                nc.tensor.transpose(bank[p][:, 0:TT], xn[:, p, 0:P], ident[0:TT, 0:TT])
                nc.tensor.transpose(bank[p][0:D1, P:P + TT], xn[:, p, P:DIM], ident[0:TT, 0:TT]).then_inc(ot_done, 1)

            pair(oproj_t, oproj)

            def n_t(t, p):
                pe.wait_ge(yn, t + 1)
                if not isinstance(t, int) or t >= 2:
                    pe.wait_ge(nt_ready, t - 1)
                nc.tensor.transpose(bank[p][:, 0:TT], xn[:, p, 0:P], ident[0:TT, 0:TT])
                nc.tensor.transpose(bank[p][0:D1, P:P + TT], xn[:, p, P:DIM], ident[0:TT, 0:TT]).then_inc(nt_done, 1)

            def n_g(t, p):
                pe.wait_ge(nt_ready, t + 1)
                if not isinstance(t, int) or t >= 2:
                    pe.wait_ge(logits_in, t - 1)
                nc.tensor.matmul(bank[2 + p][0:TT, 0:EXPERTS], xt_a[:, p, :], gatew[:, 0, :], start=True, stop=False)
                nc.tensor.matmul(bank[2 + p][0:TT, 0:EXPERTS], xt_b[0:D1, p, :], gatew[0:D1, 1, :],
                                 start=False, stop=True).then_inc(g_done, 1)

            pair(n_t, n_g)

            pe.wait_ge(tri_loaded, 16)
            pe.wait_ge(oh_ready, 1)
            for i in range(2):
                last = nc.tensor.matmul(bank[i][0:TT, 0:NT * EXPERTS], tri[:, i, :],
                                        oh[:, :, :].rearrange("p t e -> p (t e)"), start=True, stop=True)
            last.then_inc(ranked, 1)

            def ps_h(p):
                return psum[:, 3 * p:3 * p + 3, :].rearrange("p b n -> p (b n)")

            ps_t = psum[:, 6, :].bitcast(f16)
            ps_y = psum[:, 7, :]

            def slot_t(s_, p):
                pe.wait_ge(xs_in[p], 8 * (s_ - p) + 16)
                if not isinstance(s_, int) or s_ >= 1:
                    pe.wait_ge(xe, s_)
                for j in range(SUB):
                    x16 = xs[p][:, j, 0:DIM].bitcast(f16)
                    for i in range(3):
                        n = (j * 3 + i) * P
                        last = nc.tensor.transpose(ps_t[:, n:n + P], x16[:, i * P:(i + 1) * P], identh[:, :])
                last.then_inc(tt_done, 1)

            def slot_h(s_, p, w1o):
                pe.wait_ge(xe, s_ + 1)
                if not isinstance(s_, int) or s_ >= 2:
                    pe.wait_ge(gelu, s_ - 1)
                hi_a, hl_b, lo_a = (xt16[:, p, i, :] for i in range(3))
                for c in range(HC):
                    o = ps_h(p)[:, c * ST:(c + 1) * ST]
                    terms = ((w1ah, hi_a, P), (w1ah, lo_a, P), (w1al, hi_a, P), (w1bh, hl_b, P),
                             (w1bl, xl16[:, p, :], D1 + 2))
                    for n, (w, xx, k) in enumerate(terms):
                        last = nc.tensor.matmul(o, w[0:k, bass.ds(w1o + c * P, P)], xx,
                                                start=(n == 0), stop=(n == len(terms) - 1))
                last.then_inc(h_done, 1)

            def slot_y(s_, p, w2o, b2o):
                pe.wait_ge(split, s_ + 1)
                if not isinstance(s_, int) or s_ >= 1:
                    pe.wait_ge(y_ev, s_)
                for c in range(HC):
                    for a, w in ((hh[p], w2h), (hl[p], w2h), (hh[p], w2l)):
                        for j in range(SUB):
                            n = c * ST + j * P
                            nc.tensor.matmul(ps_y[:, j * DIM:(j + 1) * DIM], a[:, n:n + P],
                                             w[:, bass.ds(w2o + c * DIM, DIM)],
                                             start=(c == 0 and j == 0 and a is hh[p] and w is w2h), stop=False,
                                             skip_group_check=True)
                for j in range(SUB):
                    last = nc.tensor.matmul(ps_y[:, j * DIM:(j + 1) * DIM], ones16[:, :], b2hl[:, bass.ds(b2o, DIM)],
                                            start=False, stop=True, skip_group_check=True)
                last.then_inc(y_done, 1)

            def expert(s_):
                return pe.value_load(etab[0:1, bass.ds(s_, 1)], min_val=0, max_val=EXPERTS - 1)

            def h_step(s_, p):
                slot_h(s_, p, pe.snap(expert(s_) * HID))

            def y_step(s_, p):
                e = expert(s_)
                slot_y(s_, p, pe.snap(e * (HC * DIM)), pe.snap(e * DIM))

            pe.wait_ge(routed, 1)
            slot_t(0, 0)
            for s_ in range(2):
                slot_t(s_ + 1, 1 - s_)
                h_step(s_, s_)
            def both(s_, p):
                slot_t(s_ + 1, 1 - p)
                h_step(s_, p)
                y_step(s_ - 2, p)

            both(2, 0)
            both(3, 1)
            with pe.Fori(4, NS - 3, 2) as s_:
                both(s_, 0)
                both(s_ + 1, 1)
            slot_t(NS - 1, 1)
            h_step(NS - 2, 0)
            y_step(NS - 4, 0)
            h_step(NS - 1, 1)
            y_step(NS - 3, 1)
            y_step(NS - 2, 0)
            y_step(NS - 1, 1)

        @block.vector
        def _(dve):
            V = nc.vector

            def emb_add(t, j):
                dve.wait_ge(em_done, t + 1)
                V.tensor_tensor(h[:, bass.ds(t, 1), :].rearrange("p a d -> p (a d)"),
                                allbanks[6 + j][0:TT, 0:DIM], posb, ALU.add).then_inc(ea_done, 1)
                tile_stats(h, t, 0, ea_done, L[0]["stat"])

            def tile_stats(src, t, which, written, stat_s):
                dve.wait_ge(written, t + 1)
                dve.wait_ge(zeroed, 3)
                V.bn_stats(stats[:, which, bass.ds(t, 1)].rearrange("p a h c -> p (a h c)"),
                           src[:, bass.ds(t, 1), :].rearrange("p a d -> p (a d)")).then_inc(stat_s, 1)

            def normalise(src, t, p, which, done):
                V.tensor_scalar(xn[:, p, :], src[:, bass.ds(t, 1), :].rearrange("p a d -> p (a d)"),
                                mean[:, which, bass.ds(t, 1)],
                                rstd[:, which, bass.ds(t, 1)], ALU.subtract, ALU.mult).then_inc(done, 1)

            V.memset(qxbuf[:, :], 0.0).then_inc(zeroed, 1)
            V.memset(mx[:, :, :], 0.0).then_inc(zeroed, 1)
            V.memset(w1ah[:, 0:2 * XW], 0.0).then_inc(zeroed, 1)
            V.memset(ones16[:, :], 1.0).then_inc(small_set, 1)
            V.memset(xl16[D1:D1 + 2, :, :], XS).then_inc(small_set, 1)
            dve.wait_ge(zeroed, 3)
            dve.wait_ge(consts, CONSTS)
            V.tensor_tensor(posb, posb, bias_cls, ALU.add).then_inc(posb_ready, 1)
            V.tensor_copy(identh[:, :], ident[:, :]).then_inc(posb_ready, 1)
            dve.wait_ge(posb_ready, 2)
            with dve.Fori(0, NT - 1, 2) as t:
                emb_add(t, 0)
                emb_add(t + 1, 1)

            dve.wait_ge(late_in, 16 * 7)

            def low_halves(e):
                dve.wait_ge(w_high, e + 1)
                V.scalar_tensor_tensor(out=w1al[:, bass.ds(e * HID, HID)], in0=st_a, scalar=W1S,
                                       in1=w1ah[:, bass.ds(e * HID, HID)], op0=ALU.mult, op1=ALU.subtract)
                V.scalar_tensor_tensor(out=w2l[:, bass.ds(e * (HC * DIM), HC * DIM)], in0=st_w2, scalar=W2S,
                                       in1=w2h[:, bass.ds(e * (HC * DIM), HC * DIM)], op0=ALU.mult,
                                       op1=ALU.subtract)
                V.scalar_tensor_tensor(out=w1bl[:, bass.ds(e * HID, HID)], in0=tmp_l[:, :],
                                       scalar=neg[0:D1 + 2, 0:1], in1=st_l[0:D1 + 2], op0=ALU.mult, op1=ALU.add)
                V.scalar_tensor_tensor(out=b2hl[:, bass.ds(e * DIM, DIM)], in0=tmp_b2[:, :], scalar=neg[0:2, 1:2],
                                       in1=st_b2, op0=ALU.mult, op1=ALU.add).then_inc(w_low, 1)

            for l in range(2):
                s = L[l]
                src, which = (h, 0) if l == 0 else (xall, 2)
                if l == 1:
                    dve.wait_ge(xrstd, RSTD_OPS)
                    with dve.Fori(0, NT) as t:
                        V.tensor_scalar(xall[:, bass.ds(t, 1), :].rearrange("p a d -> p (a d)"),
                                        h[:, bass.ds(t, 1), :].rearrange("p a d -> p (a d)"),
                                        mean[:, 1, bass.ds(t, 1)],
                                        rstd[:, 1, bass.ds(t, 1)], ALU.subtract, ALU.mult).then_inc(x0, 1)
                        tile_stats(xall, t, 2, x0, s["stat"])

                def ln(t, p):
                    normalise(src, t, p, which, s["xn"])

                def xt_ev(t, p):
                    dve.wait_ge(s["t_done"], t + 1)
                    if l == 0:
                        V.tensor_copy(xt_a[:, p, :], o_ps[:, 256:256 + TT])
                        V.tensor_copy(xt_b[0:D1, p, :], o_ps[0:D1, 384:384 + TT]).then_inc(s["xt"], 1)
                    else:
                        V.tensor_scalar(xt_a[:, p, :], o_ps[:, 256:256 + TT], lnw[:, 0:1], lnw[:, 1:2],
                                        ALU.mult, ALU.add)
                        V.tensor_scalar(xt_b[0:D1, p, :], o_ps[0:D1, 384:384 + TT], lnw[0:D1, 2:3],
                                        lnw[0:D1, 3:4], ALU.mult, ALU.add).then_inc(s["xt"], 1)

                def k_ev(t, p):
                    dve.wait_ge(s["k_done"], t + 1)
                    V.tensor_copy(kt[:, p, :, :].rearrange("p m t -> p (m t)"),
                                  k_ps[:, 0:MT * TT]).then_inc(s["k_ready"], 1)

                def v_ev(t, p):
                    dve.wait_ge(s["v_done"], t + 1)
                    if not isinstance(t, int) or t >= 2:
                        dve.wait_ge(s["av"], t - 1)
                    V.tensor_copy(vt[:, p, :, :].rearrange("p h d -> p (h d)"),
                                  v_ps[0:TT, 0:HEADS * VW]).then_inc(s["v_ready"], 1)

                def maxes(t):
                    for m in range(MT):
                        dve.wait_ge(s["s_done"], 3 * t + m + 1)
                        last = V.tensor_reduce(
                            mx[:, m, :].rearrange("p (i c) -> p i c", c=SLOT)[:, :, 0:1],
                            s_ps[0:TT, m, 0:SH * TT].rearrange("p (i t) -> p i t", t=TT), AX, ALU.max, negate=True)
                    last.then_inc(s["max"], 1)

                def take(t):
                    dve.wait_ge(s["av"], t + 1)
                    o = o_ps[0:TT, 0:HEADS * VW].rearrange("p (h d) -> p h d", d=VW)
                    V.reciprocal(rs[:, :], o[:, :, HD:VW].rearrange("p h a -> p (h a)")).then_inc(s["rec"], 1)
                    dve.wait_ge(s["rec"], t + 1)
                    tile = (onorm[:, :] if l == 0 else
                            oall[:, bass.ds(t, 1), :].rearrange("p a d -> p (a d)"))
                    V.tensor_tensor(tile.rearrange("p (h d) -> p h d", d=HD), o[:, :, 0:HD],
                                    rs[:, :].rearrange("p (h a) -> p h a", a=1).to_broadcast([TT, HEADS, HD]),
                                    ALU.mult).then_inc(s["norm"], 1)
                    if l == 0:
                        dve.wait_ge(s["norm"], t + 1)
                        ht_ = h[:, bass.ds(t, 1), :].rearrange("p a d -> p (a d)")
                        V.tensor_tensor(ht_, ht_, onorm[:, :], ALU.add).then_inc(s["nrm"], 1)
                        tile_stats(h, t, 1, s["nrm"], xstat)

                def step(t, p):
                    maxes(t)
                    if inside(t, 1):
                        k_ev(t + 1, 1 - p)
                        v_ev(t + 1, 1 - p)
                    if inside(t, 2):
                        xt_ev(t + 2, p)
                    if inside(t, -1):
                        take(t - 1)
                    if inside(t, 3):
                        ln(t + 3, 1 - p)

                dve.wait_ge(s["rstd"], RSTD_OPS)
                ln(0, 0)
                ln(1, 1)
                xt_ev(0, 0)
                ln(2, 0)
                xt_ev(1, 1)
                k_ev(0, 0)
                v_ev(0, 0)
                step(0, 0)
                with dve.Fori(0, EXPERTS) as e:
                    step(2 * e + 1, 1)
                    step(2 * e + 2, 0)
                    if l == 0:
                        low_halves(e)
                for t in range(2 * EXPERTS + 1, NT):
                    step(t, t % 2)
                take(NT - 1)

            def pair(zero, first, second):
                def two(t):
                    first(t + 1, 1)
                    zero(t + 2, 0)
                    second(t, 0)
                    first(t + 2, 0)
                    zero(t + 3, 1)
                    second(t + 1, 1)

                zero(0, 0)
                zero(1, 1)
                first(0, 0)
                two(0)
                with dve.Fori(2, NT - 3, 2) as t:
                    two(t)
                first(NT - 1, 1)
                second(NT - 2, 0)
                second(NT - 1, 1)

            dve.wait_ge(L[1]["norm"], NT)

            def o_cp(t, p):
                V.tensor_copy(xn[:, p, :], oall[:, bass.ds(t, 1), :].rearrange("p a d -> p (a d)")).then_inc(nn, 1)

            def o_ev(t, p):
                dve.wait_ge(ot_done, t + 1)
                if not isinstance(t, int) or t >= 2:
                    dve.wait_ge(pj_done, t - 1)
                V.tensor_copy(xt_a[:, p, :], bank[p][:, 0:TT])
                V.tensor_copy(xt_b[0:D1, p, :], bank[p][0:D1, P:P + TT]).then_inc(ot_ready, 1)

            def o_add(t, p):
                dve.wait_ge(pj_done, t + 1)
                xs = xall[:, bass.ds(t, 1), :].rearrange("p a d -> p (a d)")
                V.tensor_tensor(xs, bank[2 + p][0:TT, 0:DIM], xs, ALU.add).then_inc(x2, 1)
                tile_stats(xall, t, 3, x2, x2stat)
                hs = h[:, bass.ds(t, 1), :].rearrange("p a d -> p (a d)")
                V.tensor_tensor(hs, hs, xs, ALU.add).then_inc(resd, 1)

            pair(o_cp, o_ev, o_add)

            dve.wait_ge(x2rstd, RSTD_OPS)
            dve.wait_ge(ln2_scaled, 1)

            def n_ln(t, p):
                if not isinstance(t, int) or t >= 2:
                    dve.wait_ge(nt_done, t - 1)
                normalise(xall, t, p, 3, ync)
                for i, op in enumerate((ALU.mult, ALU.add)):
                    dve.wait_ge(ync, 2 * t + i + 1)
                    V.tensor_tensor(xn[:, p, :], xn[:, p, :], ln2w[:, i, :], op).then_inc((ync, yn)[i], 1)
                dve.wait_ge(yn, t + 1)
                r = rows16[:, bass.ds(t, 1), :].rearrange("p a n -> p (a n)")
                V.tensor_copy(r[:, 0:DIM], xn[:, p, :]).then_inc(row_high, 1)
                dve.wait_ge(row_high, t + 1)
                V.tensor_tensor(r[:, DIM:DIM + D1], xn[:, p, P:DIM], r[:, P:DIM], ALU.subtract)
                V.tensor_tensor(r[:, DIM + D1:2 * DIM], xn[:, p, 0:P], r[:, 0:P], ALU.subtract).then_inc(row_split, 1)

            def n_ev(t, p):
                dve.wait_ge(nt_done, t + 1)
                if not isinstance(t, int) or t >= 2:
                    dve.wait_ge(g_done, t - 1)
                V.tensor_copy(xt_a[:, p, :], bank[p][:, 0:TT])
                V.tensor_copy(xt_b[0:D1, p, :], bank[p][0:D1, P:P + TT]).then_inc(nt_ready, 1)

            def n_gate(t, p):
                dve.wait_ge(g_done, t + 1)
                V.tensor_scalar(logits[:, bass.ds(t, 1), :].rearrange("p a e -> p (a e)"),
                                bank[2 + p][0:TT, 0:EXPERTS], 1.0 / XS, None, ALU.mult).then_inc(logits_in, 1)

            dve.wait_ge(resd, NT)
            pair(n_ln, n_ev, n_gate)

            chained = [0]

            def link(ins):
                ins.then_inc(gchain, 1)
                chained[0] += 1
                dve.wait_ge(gchain, chained[0])

            def wide(a):
                return a.rearrange("p (t a) -> p t a", a=1).to_broadcast([TT, NT, EXPERTS])

            def find(onehot, top_):
                link(V.tensor_reduce(top_, logits[:, :, :], AX, ALU.max))
                link(V.tensor_tensor(onehot, logits[:, :, :], wide(top_), ALU.is_equal))
                link(V.tensor_scalar(onehot, onehot, -float(EXPERTS), float(EXPERTS), ALU.mult, ALU.add))
                link(V.tensor_tensor(onehot, onehot, rc("iota"), ALU.add))
                link(V.tensor_reduce(gm[:, 3, :], onehot, AX, ALU.min))
                link(V.tensor_tensor(onehot, rc("iota"), wide(gm[:, 3, :]), ALU.is_equal))

            dve.wait_ge(logits_in, NT)
            find(first[:, :, :], gm[:, 0, :])
            link(V.tensor_scalar(second[:, :, :], first[:, :, :], -1.0, 1.0, ALU.mult, ALU.add))
            link(V.tensor_tensor(logits[:, :, :], logits[:, :, :], second[:, :, :], ALU.mult))
            link(V.tensor_scalar(second[:, :, :], first[:, :, :], -3.0e38, None, ALU.mult))
            link(V.tensor_tensor(logits[:, :, :], logits[:, :, :], second[:, :, :], ALU.add))
            find(second[:, :, :], gm[:, 1, :])
            valid = rc("valid").rearrange("p a t -> p (a t)")
            for one_hot in (first, second):
                link(V.tensor_tensor(one_hot[:, :, :], one_hot[:, :, :], wide(valid), ALU.mult))
            V.tensor_tensor(oh[:, :, :], first[:, :, :], second[:, :, :], ALU.add).then_inc(oh_ready, 1)
            V.tensor_tensor(gm[:, 1, :], gm[:, 1, :], gm[:, 0, :], ALU.subtract).then_inc(gdiff, 1)
            dve.wait_ge(gexp, 1)
            link(V.tensor_scalar(gm[:, 0, :], gm[:, 1, :], 1.0, W2S, ALU.add, ALU.mult))
            link(V.reciprocal(gm[:, 0, :], gm[:, 0, :]))
            link(V.tensor_tensor(gm[:, 1, :], gm[:, 1, :], gm[:, 0, :], ALU.mult))
            for i, rows in enumerate((rows0, rows1)):
                V.tensor_copy(rows[:, :, DIM:DIM + 1].rearrange("p t a -> p (t a)"), gm[:, i, :])
                V.tensor_copy(rows[:, :, DIM + 1:XW].rearrange("p t a -> p (t a)"), rc("dest")[:, i, :])

            tiles, before, through, start = (small[:, i, :] for i in range(4))
            dve.wait_ge(ranked, 1)
            flat = "p t e -> p (t e)"
            link(V.tensor_copy(cnt[:, :, :].rearrange(flat), bank[1][0:TT, 0:NT * EXPERTS]))
            for e in range(EXPERTS):
                last = V.tensor_tensor_scan(place[:, :, e:e + 1].rearrange("p t a -> p (t a)"),
                                            rc("ones").rearrange("p a t -> p (a t)"),
                                            cnt[:, :, e:e + 1].rearrange("p t a -> p (t a)"), 0.0,
                                            ALU.mult, ALU.add)
            link(last)

            def down(a, n):
                return a.rearrange("p (e a) -> p e a", a=1).to_broadcast([TT, EXPERTS, n])

            def across(a, rows, n):
                return a.rearrange("p (a e) -> p a e", a=1).to_broadcast([rows, n, EXPERTS])

            filled = logits[:, :, :].rearrange(flat)[:, 0:EXPERTS * MAXT].rearrange("p (e k) -> p e k", k=MAXT)
            link(V.tensor_copy(start, place[:, NT - 1, :]))
            link(V.tensor_tensor(filled, down(start, MAXT), rc("thr"), ALU.is_gt))
            link(V.tensor_reduce(tiles, filled, AX, ALU.add))
            lower = logits[:, 0:EXPERTS, :]
            link(V.tensor_tensor(lower, across(tiles, TT, EXPERTS), rc("tri8"), ALU.mult))
            link(V.tensor_reduce(before, lower, AX, ALU.add))
            link(V.tensor_tensor(through, before, tiles, ALU.add))
            link(V.tensor_scalar(start, before, float(ST), None, ALU.mult))
            link(V.tensor_tensor(place[:, :, :], place[:, :, :], cnt[:, :, :], ALU.subtract))
            link(V.tensor_tensor(place[:, :, :].rearrange(flat), bank[0][0:TT, 0:NT * EXPERTS],
                                 place[:, :, :].rearrange(flat), ALU.add))
            link(V.tensor_tensor(place[:, :, :], place[:, :, :], across(start, TT, NT), ALU.add))
            for i, one_hot in enumerate((first, second)):
                link(V.tensor_tensor(one_hot[:, :, :], one_hot[:, :, :], place[:, :, :], ALU.mult))
                link(V.tensor_reduce(gm[:, 2 + i, :], one_hot[:, :, :], AX, ALU.add))
                link(V.tensor_tensor(pos_i[:, i, :], gm[:, 2 + i, :], rc("outside").rearrange("p a t -> p (a t)"),
                                     ALU.add))
            past = etf[:, :, :]
            link(V.tensor_tensor(past, rc("tile", 1), across(through[0:1], 1, NS), ALU.is_ge))
            link(V.tensor_reduce(etn[:, :], past, AX, ALU.add))
            V.tensor_scalar(etab[:, :], etn[:, :], float(EXPERTS - 1), None, ALU.min).then_inc(routed, 1)

            def split_h(s_, p):
                dve.wait_ge(gelu, s_ + 1)
                if not isinstance(s_, int) or s_ >= 2:
                    dve.wait_ge(y_done, s_ - 1)
                V.tensor_copy(hh[p], h32).then_inc(hi_done, 1)
                dve.wait_ge(hi_done, s_ + 1)
                V.tensor_tensor(hl[p], h32, hh[p], ALU.subtract).then_inc(split, 1)

            def gate_y(s_, p):
                dve.wait_ge(y_done, s_ + 1)
                dve.wait_ge(fields_in, s_ + 1)
                if not isinstance(s_, int) or s_ >= 2:
                    dve.wait_ge(y_out[p], 8 * SUB * (s_ - p))
                V.tensor_scalar(dest[:, p, :], fields[:, bass.ds(s_, 1), :, 1:2].rearrange("p s j a -> p (s j a)"),
                                float(OUTSIDE), None, ALU.add)
                for j in range(SUB):
                    last = V.tensor_scalar(yg[:, p, j, :], psum[:, 7, j * DIM:(j + 1) * DIM],
                                           fields[:, bass.ds(s_, 1), j, 0:1].rearrange("p s a -> p (s a)"),
                                           None, ALU.mult)
                last.then_inc(y_ev, 1)

            split_h(0, 0)
            split_h(1, 1)
            gate_y(0, 0)
            split_h(2, 0)
            gate_y(1, 1)
            split_h(3, 1)
            with dve.Fori(2, NS - 3, 2) as s_:
                for p in range(2):
                    gate_y(s_ + p, p)
                    split_h(s_ + p + 2, p)
            gate_y(NS - 2, 0)
            gate_y(NS - 1, 1)

            for n, (t0, k, r) in enumerate(CHUNKS):
                dve.wait_ge(back[n], 32)
                V.tensor_tensor(h[0:r, t0:t0 + k, :], h[0:r, t0:t0 + k, :], xall[0:r, t0:t0 + k, :],
                                ALU.add).then_inc(summed, 1)
                dve.wait_ge(summed, n + 1)
                V.tensor_tensor(h[0:r, t0:t0 + k, :], h[0:r, t0:t0 + k, :], oall[0:r, t0:t0 + k, :],
                                ALU.add).then_inc(added, 1)

        @block.scalar
        def _(act):
            A = nc.scalar

            act.wait_ge(zeroed, 3)

            def high_halves(e):
                act.wait_ge(w_scaled, e + 1)
                act.wait_ge(cleared, 16)
                A.activation(w1ah[:, bass.ds(e * HID, HID)], st_a, ACT.Copy, scale=W1S)
                A.activation(w1bh[:, bass.ds(e * HID, HID)], st_b, ACT.Copy, scale=W1S)
                A.activation(w2h[:, bass.ds(e * (HC * DIM), HC * DIM)], st_w2, ACT.Copy, scale=W2S)
                A.activation(tmp_l[:, :], st_l[0:D1 + 2], ACT.Copy)
                A.activation(tmp_b2[:, :], st_b2, ACT.Copy).then_inc(w_high, 1)

            for l in range(2):
                s = L[l]

                def q_ev(t, p):
                    act.wait_ge(s["q_done"], t + 1)
                    for i in range(SH):
                        last = A.copy(qx[i * SLOT:(i + 1) * SLOT, p, :, i, :],
                                      q_ps[i * SLOT:(i + 1) * SLOT, 0:MT * TT].rearrange("p (m t) -> p m t", t=TT))
                    last.then_inc(s["q_ready"], 1)

                def m_ev(t, p):
                    act.wait_ge(s["mt_done"], t + 1)
                    for i in range(SH):
                        last = A.copy(qx[i * SLOT:i * SLOT + 1, p, :, i, :],
                                      m_ps[i * SLOT:i * SLOT + 1, 0:MT * TT].rearrange("p (m t) -> p m t", t=TT))
                    last.then_inc(s["m_ready"], 1)

                def exps(t):
                    for m in range(MT):
                        act.wait_ge(s["st_done"], 3 * t + m + 1)
                        A.activation(pt[:, m * SH:(m + 1) * SH, :].rearrange("p h t -> p (h t)"),
                                     s_ps[0:TT, m, 0:SH * TT], ACT.Exp, scale=HD ** -0.5).then_inc(s["exp"], 1)

                def step(t, p):
                    if inside(t, 1):
                        q_ev(t + 1, 1 - p)
                    m_ev(t, p)
                    exps(t)

                q_ev(0, 0)
                step(0, 0)
                with act.Fori(0, EXPERTS) as e:
                    step(2 * e + 1, 1)
                    step(2 * e + 2, 0)
                    if l == 0:
                        high_halves(e)
                for t in range(2 * EXPERTS + 1, NT):
                    step(t, t % 2)

            act.wait_ge(gdiff, 1)
            A.activation(gm[:, 1, :], gm[:, 1, :], ACT.Exp).then_inc(gexp, 1)

            def slot_ev(s_, p):
                act.wait_ge(tt_done, s_ + 1)
                if not isinstance(s_, int) or s_ >= 2:
                    act.wait_ge(h_done, s_ - 1)
                src = psum[:, 6, :].bitcast(f16)[:, 0:3 * ST].rearrange("p (j i n) -> p i j n", j=SUB, i=3)
                A.copy(xt16[:, p, :, :].rearrange("p i (j n) -> p i j n", j=SUB), src)
                A.copy(xl16[0:D1, p, :].rearrange("p (j n) -> p j n", j=SUB), src[0:D1, 1]).then_inc(xe, 1)

            def hidden(s_, p):
                act.wait_ge(h_done, s_ + 1)
                if not isinstance(s_, int) or s_ >= 1:
                    act.wait_ge(split, s_)
                A.activation(h32, psum[:, 3 * p:3 * p + 3, :].rearrange("p b n -> p (b n)"), ACT.Gelu, scale=1.0 / (XS * W1S)).then_inc(gelu, 1)

            slot_ev(0, 0)
            slot_ev(1, 1)
            hidden(0, 0)
            slot_ev(2, 0)
            hidden(1, 1)
            slot_ev(3, 1)
            with act.Fori(2, NS - 3, 2) as s_:
                for p in range(2):
                    hidden(s_ + p, p)
                    slot_ev(s_ + p + 2, p)
            hidden(NS - 2, 0)
            hidden(NS - 1, 1)

        @block.gpsimd
        def _(pool):
            pool.memset(half[:, :], -0.5).then_inc(half_set, 1)
            pool.wait_ge(half_set, 1)
            def alone(s_, value):
                value = value if isinstance(value, int) else pool.to_reg(value)
                pool.wait_ge(late_in, 16 * 7)
                pool.wait_ge(s_, value)

            pool.wait_ge(late_in, 16 * 7)
            pool.tensor_scalar(ln2w[:, :, :], ln2w[:, :, :], XS, None, ALU.mult).then_inc(ln2_scaled, 1)
            for which, stat_s, done in ((0, L[0]["stat"], L[0]["rstd"]), (1, xstat, xrstd),
                                        (2, L[1]["stat"], L[1]["rstd"]), (3, x2stat, x2rstd)):
                pool.wait_ge(stat_s, NT)

                def col(h_, c):
                    return stats[:, which, :, h_, c:c + 1].rearrange("p t a -> p (t a)")

                var = rstd[:, which, :]
                steps = (
                    lambda: pool.tensor_tensor(mean[:, which, :], col(0, 1), col(1, 1), ALU.add),
                    lambda: pool.tensor_scalar(mean[:, which, :], mean[:, which, :], 0.5, None, ALU.mult),
                    lambda: pool.tensor_tensor(gap[:, :], col(0, 1), mean[:, which, :], ALU.subtract),
                    lambda: pool.tensor_tensor(gap[:, :], gap[:, :], gap[:, :], ALU.mult),
                    lambda: pool.tensor_tensor(var, col(0, 2), col(1, 2), ALU.add),
                    lambda: pool.tensor_scalar(var, var, 1.0 / DIM, EPS, ALU.mult, ALU.add),
                    lambda: pool.tensor_tensor(var, var, gap[:, :], ALU.add),
                    lambda: pool.tensor_tensor(var, var, half[:, :], ALU.pow),
                )
                for n, op in enumerate(steps):
                    op().then_inc(done, 1)
                    if n + 1 < len(steps):
                        pool.wait_ge(done, n + 1)
                if which == 0:
                    with pool.Fori(0, EXPERTS) as e:
                        alone(w_in, 16 * PREP * (e + 1))
                        pool.tensor_scalar(st_l[0:D1 + 2], st_l[0:D1 + 2], W1S, None, ALU.mult)
                        pool.tensor_scalar(st_b2, st_b2, W2S, None, ALU.mult).then_inc(w_scaled, 1)

            with pool.Fori(0, NT) as t:
                alone(row_split, t + 1)
                pool.tensor_copy(rows1[:, bass.ds(t, 1), 0:DIM].rearrange("p a n -> p (a n)"),
                                 rows0[:, bass.ds(t, 1), 0:DIM].rearrange("p a n -> p (a n)")).then_inc(row_copied, 1)

            pool.wait_ge(routed, 1)
            pool.wait_ge(cleared, 16)
            pool.wait_ge(row_copied, NT)
            for t in range(NT):
                for i, rows in enumerate((rows0, rows1)):
                    pool.indirect_dma_start(slots, bass.IndirectOffsetOnAxis(ap=pos_i[:, i, t:t + 1], axis=0),
                                            rows[:, t, :], None, bounds_check=NSLOT - 1,
                                            oob_is_err=False).then_inc(scattered, 16)

            def take_fields(s_, p):
                alone(xs_in[p], 8 * (s_ - p) + 16)
                pool.tensor_copy(fields[:, bass.ds(s_, 1), :, :].rearrange("p s j a -> p (s j) a"),
                                 xs[p][:, :, DIM:XW]).then_inc(fields_in, 1)

            def scatter_y(s_, p):
                alone(y_ev, s_ + 1)
                for j in range(SUB):
                    pool.indirect_dma_start(ymoe, bass.IndirectOffsetOnAxis(ap=dest[:, p, j:j + 1], axis=0),
                                            yg[:, p, j, :], None, bounds_check=last_row,
                                            oob_is_err=False).then_inc(y_out[p], 16)

            last_row = pool.to_reg(2 * NT * TT - 1)
            for s_ in range(AHEAD):
                take_fields(s_, s_ % 2)
            for s_ in range(2):
                take_fields(s_ + AHEAD, s_ % 2)
                scatter_y(s_, s_ % 2)
            with pool.Fori(2, NS - AHEAD - 1, 2) as s_:
                for p in range(2):
                    take_fields(s_ + p + AHEAD, p)
                    scatter_y(s_ + p, p)
            for s_ in range(NS - AHEAD, NS):
                scatter_y(s_, s_ % 2)


def _slots(wa, ba, wb, bb):
    w = np.zeros((DIM + 4, 2, MT, SH, SLOT), np.float32)
    for n, (wm, bm) in enumerate(((wa, ba), (wb, bb))):
        w[:DIM, n, :, :, 4:4 + HD] = wm.reshape(DIM, MT, SH, HD)
        w[DIM, n, :, :, 4:4 + HD] = bm.reshape(MT, SH, HD)
    w[DIM, 1, :, :, 0] = 1.0
    for i in range(TI):
        w[DIM + 1 + i, 0, :, :, 1 + i] = 1.0
        w[DIM, 1, :, :, 1 + i] = -BIG
        w[DIM + 1 + i, 1, :, :, 1 + i] = BIG
    return w.reshape(DIM + 4, 2 * MT * P)


def _values(wm, bm):
    w = np.zeros((DIM + 4, HEADS, VW), np.float32)
    w[:DIM, :, :HD] = wm.reshape(DIM, HEADS, HD)
    w[DIM, :, :HD] = bm.reshape(HEADS, HD)
    w[DIM, :, HD] = 1.0
    return w.reshape(DIM + 4, HEADS * VW)


def kernel(**inputs):
    import concourse.bacc as bacc
    from concourse.bass_utils import run_bass_kernel_spmd

    a = {k: np.asarray(v) for k, v in inputs.items()}
    qkv_w = a["L0_ffn_qkv_w"].reshape(DIM, 3, DIM)
    qkv_b = a["L0_ffn_qkv_b"].reshape(3, DIM)
    qk = np.stack([_slots(a["L0_attn_Wq"].T, a["L0_attn_bq"], a["L0_attn_Wk"].T, a["L0_attn_bk"]),
                   _slots(qkv_w[:, 0], qkv_b[0], qkv_w[:, 1], qkv_b[1])])
    vv = np.stack([_values(a["L0_attn_Wv"].T, a["L0_attn_bv"]), _values(qkv_w[:, 2], qkv_b[2])])

    def ln(g, b):
        w = np.zeros((P, 4), np.float32)
        w[:, 0], w[:, 1] = g[:P], b[:P]
        w[:D1, 2], w[:D1, 3] = g[P:], b[P:]
        return w

    token = np.arange(NT)[None] * TT + np.arange(TT)[:, None]
    real = (token < IMAGES * TOK).astype(np.float32)
    route = np.concatenate([
        np.tile(np.arange(EXPERTS), (TT, NT)), np.tile(np.arange(MAXT) * ST, (TT, EXPERTS)),
        np.tile((np.arange(EXPERTS)[None] < np.arange(EXPERTS)[:, None]).reshape(1, -1), (TT, 1)),
        np.tile(np.repeat(np.arange(NS), EXPERTS)[None], (TT, 1)),
        token - OUTSIDE, token + NT * TT - OUTSIDE, (1 - real) * OUTSIDE, real, np.ones((TT, NT)),
    ], axis=1).astype(np.float32)
    tri = np.stack([np.triu(np.ones((TT, TT), np.float32), 1), np.ones((TT, TT), np.float32)], axis=1)
    neg = np.zeros((P, 2), np.float32)
    neg[:, 0] = -1.0
    neg[D1, 0] = 0.0
    neg[1, 1] = -1.0
    aug = np.zeros((4, NT * TT), np.float32)
    aug[0] = 1.0
    for i in range(TI):
        aug[1 + i] = np.tile(np.repeat(np.arange(TI) == i, TOK), NT)
    pt = a["x"].reshape(IMAGES, CHANNELS, PER_SIDE, PATCH, PER_SIDE, PATCH).transpose(0, 1, 2, 4, 3, 5)
    px = np.zeros((NT * TI, TOK, PIX), np.float32)
    px[:IMAGES, 1:] = pt.reshape(IMAGES, PATCHES, PIX)
    px = px.reshape(NG, GT, TT, KC, P).transpose(0, 4, 1, 3, 2).reshape(NG, P, GT * KC * TT)
    arrays = {
        "x": px, "pos": a["L0_tok_pos_embedding"],
        "tok_b": np.repeat(a["L0_tok_b"].reshape(1, DIM), TT, 0), "cls": a["L0_tok_class_token"],
        "w_emb": a["L0_tok_W"].T,
        "wqk_a": qk[:, :P], "wqk_b": qk[:, P:], "wv_a": vv[:, :P], "wv_b": vv[:, P:],
        "ln1": ln(a["L0_ffn_ln1_g"], a["L0_ffn_ln1_b"]),
        "ln2_g": np.repeat(a["L0_ffn_ln2_g"].reshape(1, DIM), TT, 0),
        "ln2_b": np.repeat(a["L0_ffn_ln2_b"].reshape(1, DIM), TT, 0),
        "proj": np.concatenate([a["L0_ffn_proj_w"], a["L0_ffn_proj_b"].reshape(1, DIM)]),
        "gate": a["L0_ffn_gate_w"], "w1": a["L0_ffn_w1"], "b1": a["L0_ffn_b1"],
        "w2": a["L0_ffn_w2"], "b2": a["L0_ffn_b2"],
        "ident": np.eye(P, dtype=np.float32), "aug": aug,
        "route": route, "tri": tri, "neg": neg,
    }
    arrays = {k: np.ascontiguousarray(v) for k, v in arrays.items()}
    nc = bacc.Bacc("TRN2", target_bir_lowering=False, num_devices=1)
    args = [nc.dram_tensor(f"in_{k}", v.shape, mybir.dt.from_np(v.dtype), kind="ExternalInput").ap()
            for k, v in arrays.items()]
    args.append(nc.dram_tensor("slots", (NSLOT, XW), mybir.dt.float32, kind="Internal").ap())
    args.append(nc.dram_tensor("ymoe", (2 * NT * TT, DIM), mybir.dt.float32, kind="Internal").ap())
    out = nc.dram_tensor("out", (NT, TT, DIM), mybir.dt.float32, kind="ExternalOutput").ap()
    build(nc, *args, out)
    r = run_bass_kernel_spmd(nc, [{f"in_{k}": v for k, v in arrays.items()}], core_ids=[0])
    return r.results[0]["out"].reshape(NT * TT, DIM)[:IMAGES * TOK].reshape(IMAGES, TOK, DIM)
```

```python
import numpy as np
import concourse.bass as bass
from concourse import mybir
from contextlib import ExitStack

IMAGES, CHANNELS, SIDE, PATCH = 64, 3, 96, 16
PER_SIDE = SIDE // PATCH
PATCHES = PER_SIDE * PER_SIDE
TOK = PATCHES + 1
DIM, HEADS = 192, 12
HD = DIM // HEADS
EXPERTS, HID = 8, 768
PIX = CHANNELS * PATCH * PATCH
P = 128
TI = 3
TT = TI * TOK
NT = -(-IMAGES // TI)
TAIL = (IMAGES - (NT - 1) * TI) * TOK
GT = 2
NG = NT // GT
KC = PIX // P
D1 = DIM - P
AUG = D1 + 4
SLOT = 32
SH = P // SLOT
MT = HEADS // SH
VW = HD + 1
BIG = float(2 ** 40)
EPS = 1e-5
HC = HID // P
SUB = 2
ST = SUB * P
NS = (2 * IMAGES * TOK + EXPERTS * (ST - 1)) // ST
NSLOT = NS * ST
XW = DIM + 2
OUTSIDE = 8192
MAXT = -(-IMAGES * TOK // ST)
XS, W1S, W2S = 16.0, 256.0, 256.0
LE = EXPERTS // 2
AHEAD = 4
PREP = 9
CHUNKS = ((0, 6, TT), (6, 6, TT), (12, 5, TT), (17, NT - 18, TT), (NT - 1, 1, TAIL))


def inside(t, off):
    return not isinstance(t, int) or 0 <= t + off < NT


def build(nc, x, pos, tok_b, cls, w_emb, wqk_a, wqk_b, wv_a, wv_b, ln1, ln2_g, ln2_b, proj, gate, w1, b1, w2, b2,
          ident_in, aug_in, route_in, tri_in, keep_in, slots, ymoe, out):
    f32 = mybir.dt.float32
    i32, f16 = mybir.dt.int32, mybir.dt.float16
    ALU, ACT, AX = mybir.AluOpType, mybir.ActivationFunctionType, mybir.AxisListType.X
    ctx = ExitStack()
    with ctx:
        def sb(name, shape, dt=f32):
            return ctx.enter_context(nc.sbuf_tensor(name, shape, dt))

        def sem(name):
            return ctx.enter_context(nc.semaphore(name))

        ident = sb("ident", [P, P])
        posbuf = sb("posbuf", [TT, 2 * DIM])
        posb, bias_cls = posbuf[:, 0:DIM], posbuf[:, DIM:2 * DIM]
        wqka = sb("wqka", [P, 2, 2 * MT * P])
        wqkb = sb("wqkb", [P, 2, 2 * MT * P])
        wva = sb("wva", [P, 2, HEADS * VW])
        wvb = sb("wvb", [AUG, 2, HEADS * VW])
        lnw = sb("lnw", [P, 4])
        gatew = sb("gatew", [P, 2, EXPERTS])
        keep_low = sb("keep_low", [P, 2])
        embbuf = sb("embbuf", [P, 2 * GT * KC * TT + KC * DIM])
        patches = embbuf[:, 0:2 * GT * KC * TT].rearrange("p (b g c t) -> p b g c t", b=2, g=GT, c=KC)
        wemb = embbuf[:, 2 * GT * KC * TT:].rearrange("p (c d) -> p c d", d=DIM)
        st_a, st_b, st_l = (embbuf[:, i * HID:(i + 1) * HID] for i in range(3))
        st_w2 = embbuf[:, 3 * HID:3 * HID + HC * DIM]
        st_b2 = embbuf[0:2, 3 * HID + HC * DIM:3 * HID + HC * DIM + DIM]
        tmp_l = sb("tmp_l", [D1 + 2, HID], f16)
        tmp_b2 = sb("tmp_b2", [2, DIM], f16)
        w1ah = sb("w1ah", [P, EXPERTS * HID], f16)
        w1al = sb("w1al", [P, EXPERTS * HID], f16)
        w1bh = sb("w1bh", [P, EXPERTS * HID], f16)
        w1bl = sb("w1bl", [D1 + 2, EXPERTS * HID], f16)
        w2h = sb("w2h", [P, EXPERTS * HC * DIM], f16)
        w2l = sb("w2l", [P, EXPERTS * HC * DIM], f16)
        b2hl = sb("b2hl", [2, EXPERTS * DIM], f16)
        h = sb("h", [TT, NT, DIM])
        rows0 = sb("rows0", [TT, NT, XW])
        rows1 = sb("rows1", [TT, NT, XW])
        xall, oall = rows0[:, :, 0:DIM], rows1[:, :, 0:DIM]
        rows16, rows16_1 = (r[:, :, 0:DIM].bitcast(f16) for r in (rows0, rows1))
        stats = sb("stats", [TT, 4, 2, 6])
        meanvar = sb("meanvar", [TT, 4, 2, 2])
        vareps = sb("vareps", [TT, 4, 2])
        mean = sb("mean", [TT, 4, NT])
        rstd = sb("rstd", [TT, 4, NT])
        half = sb("half", [TT, 1])
        xn = sb("xn", [TT, 2, DIM])
        xt_a = sb("xt_a", [P, 2, TT])
        xt_b = sb("xt_b", [AUG, 2, TT])
        qxbuf = sb("qxbuf", [P, 2 * MT * SH * TT])
        qx = qxbuf[:, :].rearrange("p (b m i t) -> p b m i t", b=2, m=MT, i=SH)
        ktbuf = sb("ktbuf", [P, 2 * MT * TT])
        kt = ktbuf[:, :].rearrange("p (b m t) -> p b m t", b=2, m=MT)
        vt = sb("vt", [TT, 2, HEADS, 2 * VW], f16)
        mx = sb("mx", [TT, P])
        ptbuf = sb("ptbuf", [P, HEADS * TT])
        pt_high, pt_low = (ptbuf[0:TT, i * HEADS * TT // 2:(i + 1) * HEADS * TT // 2].bitcast(f16).rearrange(
            "p (h t) -> p h t", t=TT) for i in range(2))
        pt32 = sb("pt32", [TT, MT, SH * TT])
        osum = sb("osum", [TT, HEADS, VW])
        rs = sb("rs", [TT, HEADS])
        onorm = sb("onorm", [TT, DIM])
        spare = wqka[:, :, :].rearrange("p l n -> p (l n)")
        NE = NT * EXPERTS
        first, second, oh, cnt, place, logits = (
            spare[0:TT, i * NE:(i + 1) * NE].rearrange("p (t e) -> p t e", e=EXPERTS) for i in range(6))
        etf = wva[0:1, :, :].rearrange("p l n -> p (l n)")[:, 0:NS * EXPERTS].rearrange(
            "p (s e) -> p s e", e=EXPERTS)
        gm = sb("gm", [TT, 4, NT])
        pos_i = sb("pos_i", [TT, 2, NT], i32)
        small = sb("small", [TT, 4, EXPERTS])
        etab = sb("etab", [1, NS], i32)
        etn = sb("etn", [1, NS])
        RC = {}
        at = 0
        for name, shape in (("iota", (NT, EXPERTS)), ("thr", (EXPERTS, MAXT)), ("tri8", (EXPERTS, EXPERTS)),
                            ("tile", (NS, EXPERTS)), ("dest", (2, NT)), ("outside", (1, NT)), ("valid", (1, NT)),
                            ("ones", (1, NT))):
            RC[name] = (at, shape)
            at += shape[0] * shape[1]
        wqkb_flat = wqkb[:, :, :].rearrange("p l n -> p (l n)")
        route = wqkb_flat[0:TT, 0:at]
        projw = wqkb_flat[:, at:at + 2 * DIM].rearrange("p (c d) -> p c d", d=DIM)
        ln2w = spare[0:TT, 6 * NE:6 * NE + 2 * DIM].rearrange("p (c d) -> p c d", d=DIM)

        def rc(name, rows=TT):
            o, (a, b) = RC[name]
            return route[0:rows, o:o + a * b].rearrange("p (a b) -> p a b", b=b)

        tri = posbuf[:, 0:2 * TT].rearrange("p (a t) -> p a t", a=2)
        h32 = qxbuf[:, 0:HC * ST]
        hh = [qxbuf[:, HC * ST:HC * ST * 3 // 2].bitcast(f16), ptbuf[:, 0:HC * ST // 2].bitcast(f16)]
        hl = [wqkb[:, :, :].rearrange("p l n -> p (l n)")[:, i * HC * ST // 2:(i + 1) * HC * ST // 2].bitcast(f16)
              for i in range(2)]
        xs = [v.rearrange("p (j n) -> p j n", j=SUB)
              for v in (ptbuf[:, HC * ST // 2:HC * ST // 2 + SUB * XW], ktbuf[:, 0:SUB * XW])]
        yg = spare[:, 0:2 * SUB * DIM].rearrange("p (b j d) -> p b j d", b=2, j=SUB)
        xt16 = spare[:, 2 * SUB * DIM:4 * SUB * DIM].bitcast(f16).rearrange("p (b i n) -> p b i n", b=2, i=3)
        xl16 = sb("xl16", [D1 + 2, 2, ST], f16)
        ones16 = sb("ones16", [2, P], f16)
        identh = sb("identh", [P, P], f16)
        dest = sb("dest", [P, 2, SUB], i32)
        fields = sb("fields", [P, NS, SUB, 2])

        psum = ctx.enter_context(nc.psum_tensor("psum", [P, 8, 512], f32))
        bank = [psum[:, i, :] for i in range(5)]
        s_ps = psum[:, 5:8, :]
        allbanks = [psum[:, i, :] for i in range(8)]
        v_ps, q_ps, k_ps, o_ps, m_ps = bank

        def maxima(i):
            return m_ps[i * SLOT:i * SLOT + MT, 0:TT].rearrange("p (a t) -> p a t", a=1).to_broadcast([MT, MT, TT])

        consts = sem("consts")
        wemb_in, wqkv_in, late_in, end_in = sem("wemb_in"), sem("wqkv_in"), sem("late_in"), sem("end_in")
        x_in = [sem("x_in0"), sem("x_in1")]
        zeroed, posb_a, posb_ready = sem("zeroed"), sem("posb_a"), sem("posb_ready")
        half_set = sem("half_set")
        em_done, ea_done = sem("em_done"), sem("ea_done")
        block = ctx.enter_context(nc.Block())

        L = [dict((n, sem(f"{n}_{l}")) for n in (
            "xn", "t_done", "xt", "q_done", "k_done", "v_done", "q_ready", "k_ready",
            "v_ready", "s_done", "max", "mt_done", "m_ready", "m_ready2",
            "st_done", "exp", "low", "av", "v_high", "part", "osum", "rec", "norm"))
            for l in range(2)]
        stat, aggr, eps_in, rstd_in = ([sem(f"{n}{i}") for i in range(4)]
                                       for n in ("stat", "aggr", "eps_in", "rstd_in"))
        x0, h_in = sem("x0"), sem("h_in")
        ot_done, ot_ready, pj_done, x2, resd = (
            sem(n) for n in ("ot_done", "ot_ready", "pj_done", "x2", "resd"))
        nn, nt_done, nt_ready, g_done, logits_in, gchain, gdiff, gexp = (
            sem(n) for n in ("nn", "nt_done", "nt_ready", "g_done", "logits_in", "gchain", "gdiff", "gexp"))
        w_in, w_high, w_low = sem("w_in"), sem("w_high"), sem("w_low")
        ln2_scaled, yn, ync, row_split, row_copied = (
            sem(n) for n in ("ln2_scaled", "yn", "ync", "row_split", "row_copied"))
        tri_loaded = sem("tri_loaded")
        row_high = sem("row_high")
        oh_ready, ranked, routed, cleared, scattered, ones_set = (
            sem(n) for n in ("oh_ready", "ranked", "routed", "cleared", "scattered", "ones_set"))
        xs_in = [sem("xs_in0"), sem("xs_in1")]
        y_out = [sem("y_out0"), sem("y_out1")]
        tt_done, xe, h_done, gelu, hi_done, split, y_done, y_ev, fields_in = (
            sem(n) for n in ("tt_done", "xe", "h_done", "gelu", "hi_done", "split", "y_done", "y_ev", "fields_in"))
        back = [sem(f"back{i}") for i in range(len(CHUNKS))]
        summed, added, stored = sem("summed"), sem("added"), sem("stored")

        CONSTS = 16 * (1 + 2 * TI + 2 + 1)

        @block.sync
        def _(sp):
            def load_group(g, p):
                sp.dma_start(patches[:, p].rearrange("p g c t -> p (g c t)"),
                             x[bass.ds(g, 1), :, :].rearrange("a p n -> (a p) n")).then_inc(x_in[p], 16)

            sp.dma_start(wemb[:, :, :], w_emb.rearrange("(c p) d -> p c d", p=P)).then_inc(wemb_in, 16)
            load_group(0, 0)
            sp.dma_start(ident[:, :], ident_in).then_inc(consts, 16)
            for i in range(TI):
                sp.dma_start(posb[i * TOK:(i + 1) * TOK, :], pos).then_inc(consts, 16)
            sp.dma_start(bias_cls, tok_b).then_inc(posb_a, 16)
            sp.wait_ge(posb_a, 16)
            for i in range(TI):
                sp.dma_start(bias_cls[i * TOK:i * TOK + 1, :], cls).then_inc(consts, 16)
            load_group(1, 1)
            for i in range(2):
                sp.dma_start(xt_b[D1:AUG, i, :], aug_in[:, 0:TT]).then_inc(consts, 16)
            sp.dma_start(keep_low[:, :], keep_in).then_inc(consts, 16)
            sp.dma_start(wqka[:, :, :], wqk_a.rearrange("l p n -> p l n")).then_inc(wqkv_in, 16)
            sp.dma_start(wqkb[0:AUG, :, :], wqk_b.rearrange("l p n -> p l n")).then_inc(wqkv_in, 16)
            sp.dma_start(wva[:, :, :], wv_a.rearrange("l p n -> p l n")).then_inc(wqkv_in, 16)
            sp.dma_start(wvb[:, :, :], wv_b.rearrange("l p n -> p l n")).then_inc(wqkv_in, 16)
            sp.dma_start(lnw[:, :], ln1).then_inc(late_in, 16)
            sp.dma_start(gatew[:, 0, :], gate[0:P, :]).then_inc(late_in, 16)
            sp.dma_start(gatew[0:D1, 1, :], gate[P:, :]).then_inc(late_in, 16)
            with sp.Fori(2, NG - 1, 2) as g:
                for p in range(2):
                    sp.wait_ge(em_done, (g + p - 1) * GT)
                    load_group(g + p, p)
            sp.wait_ge(em_done, (NG - 2) * GT)
            load_group(NG - 1, 0)

            sp.wait_ge(zeroed, 3)
            zeros = w1ah[:, 0:2 * XW].bitcast(f32).rearrange("p (a n) -> p a n", a=1)
            sp.dma_start(slots.rearrange("(s p) n -> p s n", p=P),
                         zeros.to_broadcast([P, SUB * NS, XW])).then_inc(cleared, 16)

            def load_expert(e):
                for dst, src in ((st_a, w1[bass.ds(e, 1), 0:P, :]), (st_b[0:D1], w1[bass.ds(e, 1), P:, :]),
                                 (st_b[D1:P], w1[bass.ds(e, 1), P:, :]), (st_l[0:D1], w1[bass.ds(e, 1), P:, :])):
                    sp.dma_start(dst, src.rearrange("a p n -> (a p) n")).then_inc(w_in, 16)
                for i in range(2):
                    sp.dma_start(st_l[D1 + i:D1 + i + 1], b1[bass.ds(e, 1), :]).then_inc(w_in, 16)
                    sp.dma_start(st_b2[i:i + 1], b2[bass.ds(e, 1), :]).then_inc(w_in, 16)
                sp.dma_start(st_w2.rearrange("p (c d) -> p c d", d=DIM),
                             w2[bass.ds(e, 1)].rearrange("a (c p) d -> p (a c) d", p=P)).then_inc(w_in, 16)

            sp.wait_ge(em_done, NT)
            sp.wait_ge(ea_done, NT)
            sp.dma_start(tri, tri_in).then_inc(tri_loaded, 16)
            load_expert(0)
            with sp.Fori(1, EXPERTS) as e:
                sp.wait_ge(w_low, e)
                load_expert(e)

            sp.wait_ge(L[1]["v_done"], NT)
            sp.dma_start(projw[:, 0, :], proj[0:P, :]).then_inc(end_in, 16)
            sp.dma_start(projw[0:D1 + 1, 1, :], proj[P:, :]).then_inc(end_in, 16)
            sp.dma_start(ln2w[:, 0, :], ln2_g).then_inc(end_in, 16)
            sp.dma_start(ln2w[:, 1, :], ln2_b).then_inc(end_in, 16)
            sp.dma_start(route, route_in).then_inc(end_in, 16)

            def load_slots(s_, p):
                sp.dma_start(xs[p], slots[bass.ds(s_ * ST, ST), :].rearrange("(j p) n -> p j n", p=P)
                             ).then_inc(xs_in[p], 16)

            sp.wait_ge(scattered, 16 * 2 * NT)
            load_slots(0, 0)
            load_slots(1, 1)
            with sp.Fori(2, NS - 1, 2) as s_:
                for p in range(2):
                    sp.wait_ge(tt_done, s_ + (p - 1))
                    sp.wait_ge(fields_in, s_ + (p - 1))
                    load_slots(s_ + p, p)

            for p in range(2):
                sp.wait_ge(y_out[p], 16 * SUB * NS // 2)
            for n, (t0, k, r) in enumerate(CHUNKS):
                for i, dst in enumerate((xall, oall)):
                    sp.dma_start(dst[0:r, t0:t0 + k, :],
                                 ymoe[(i * NT + t0) * TT:(i * NT + t0) * TT + (k - 1) * TT + r, :].rearrange(
                                     "(t p) d -> p t d", p=r)).then_inc(back[n], 16)
            for n, (t0, k, r) in enumerate(CHUNKS):
                sp.wait_ge(added, n + 1)
                sp.dma_start(out[t0:t0 + k, 0:r, :].rearrange("t p d -> p t d"), h[0:r, t0:t0 + k, :]
                             ).then_inc(stored, 16)
            sp.wait_ge(stored, 16 * len(CHUNKS))

        @block.tensor
        def _(pe):
            def embed(g, p):
                pe.wait_ge(x_in[p], 8 * (g - p) + 16)
                for j in range(GT):
                    if not isinstance(g, int) or g >= 1:
                        pe.wait_ge(ea_done, g * GT + j - 1)
                    for c in range(KC):
                        last = nc.tensor.matmul(allbanks[6 + j % 2][0:TT, 0:DIM],
                                                patches[:, p, j, c, :], wemb[:, c, :],
                                                start=(c == 0), stop=(c == KC - 1))
                    last.then_inc(em_done, 1)

            pe.wait_ge(wemb_in, 16)
            embed(0, 0)
            with pe.Fori(1, NG - 1, 2) as g:
                embed(g, 1)
                embed(g + 1, 0)

            pe.wait_ge(consts, CONSTS)
            pe.wait_ge(wqkv_in, 64)
            for l in range(2):
                s = L[l]

                def tr(t, p, s=s):
                    pe.wait_ge(s["xn"], t + 1)
                    if not isinstance(t, int) or t >= 1:
                        pe.wait_ge(s["v_ready"], t)
                    nc.tensor.transpose(v_ps[:, 256:256 + TT], xn[:, p, 0:P], ident[0:TT, 0:TT])
                    nc.tensor.transpose(v_ps[0:D1, 384:384 + TT], xn[:, p, P:DIM],
                                        ident[0:TT, 0:TT]).then_inc(s["t_done"], 1)

                def qkv(t, p, l=l, s=s):
                    pe.wait_ge(s["xt"], t + 1)
                    for o, ps, name in ((0, q_ps, "q_done"), (MT, k_ps, "k_done")):
                        for m in range(MT):
                            c0 = (o + m) * P
                            nc.tensor.matmul(ps[:, m * TT:(m + 1) * TT], wqka[:, l, c0:c0 + P], xt_a[:, p, :],
                                             start=True, stop=False)
                            last = nc.tensor.matmul(ps[:, m * TT:(m + 1) * TT], wqkb[0:AUG, l, c0:c0 + P],
                                                    xt_b[:, p, :], start=False, stop=True)
                        last.then_inc(s[name], 1)
                    if not isinstance(t, int) or t >= 1:
                        pe.wait_ge(s["v_ready"], t)
                    nc.tensor.matmul(v_ps[0:TT, 0:HEADS * VW], xt_a[:, p, :], wva[:, l, :], start=True, stop=False)
                    nc.tensor.matmul(v_ps[0:TT, 0:HEADS * VW], xt_b[:, p, :], wvb[:, l, :], start=False,
                                     stop=True).then_inc(s["v_done"], 1)

                def scores(t, p):
                    pe.wait_ge(s["q_ready"], t + 1)
                    pe.wait_ge(s["k_ready"], t + 1)
                    for m in range(MT):
                        if not isinstance(t, int) or t >= 1:
                            pe.wait_ge(s["exp"], 3 * t - 2 + m)
                        for i in range(SH):
                            last = nc.tensor.matmul(s_ps[0:TT, m, i * TT:(i + 1) * TT], qx[:, p, m, i, :],
                                                    kt[:, p, m, :], start=True, stop=True)
                        last.then_inc(s["s_done"], 1)

                def max_t(t):
                    pe.wait_ge(s["max"], t + 1)
                    nc.tensor.transpose(m_ps[:, 0:TT], mx[:, :], ident[0:TT, 0:TT]).then_inc(s["mt_done"], 1)

                def scores_t(t, p):
                    pe.wait_ge(s["m_ready"], t + 1)
                    pe.wait_ge(s["m_ready2"], t + 1)
                    for m in range(MT):
                        nc.tensor.matmul(s_ps[0:TT, m, 0:SH * TT], kt[:, p, m, :],
                                         qx[:, p, m, :, :].rearrange("p i t -> p (i t)"),
                                         start=True, stop=True).then_inc(s["st_done"], 1)

                def attend(t, p):
                    pe.wait_ge(s["low"], 3 * t + 3)
                    pe.wait_ge(s["v_ready"], t + 1)
                    if not isinstance(t, int) or t >= 1:
                        pe.wait_ge(s["norm"], t)
                    for hd in range(HEADS):
                        c = hd * 2 * VW
                        nc.tensor.matmul(o_ps[0:TT, c:c + 2 * VW], pt_high[:, hd, :], vt[:, p, hd, :],
                                         start=True, stop=False, skip_group_check=True)
                        last = nc.tensor.matmul(o_ps[0:TT, c + VW:c + 2 * VW], pt_low[:, hd, :], vt[:, p, hd, 0:VW],
                                                start=False, stop=True, skip_group_check=True)
                    last.then_inc(s["av"], 1)

                def step(t, p):
                    scores(t, p)
                    if inside(t, 1):
                        qkv(t + 1, 1 - p)
                    max_t(t)
                    if inside(t, -1):
                        attend(t - 1, 1 - p)
                    scores_t(t, p)
                    if inside(t, 2):
                        tr(t + 2, p)

                if l == 0:
                    tr(0, 0)
                    qkv(0, 0)
                tr(1, 1)
                step(0, 0)
                with pe.Fori(1, NT - 4, 2) as t:
                    step(t, 1)
                    step(t + 1, 0)
                for t in range(NT - 3, NT):
                    step(t, t % 2)
                if l == 0:
                    pe.wait_ge(s["v_ready"], NT)
                    tr(0, 0, L[1])
                    qkv(0, 0, 1, L[1])
                attend(NT - 1, 1)

            pe.wait_ge(late_in, 16 * 3)
            pe.wait_ge(end_in, 16 * 5)

            def oproj(t, p):
                pe.wait_ge(ot_ready, t + 1)
                if not isinstance(t, int) or t >= 2:
                    pe.wait_ge(x2, t - 1)
                nc.tensor.matmul(bank[2 + p][0:TT, 0:DIM], xt_a[:, p, :], projw[:, 0, :], start=True, stop=False)
                nc.tensor.matmul(bank[2 + p][0:TT, 0:DIM], xt_b[0:D1 + 1, p, :], projw[0:D1 + 1, 1, :],
                                 start=False, stop=True).then_inc(pj_done, 1)

            def pair(first, second):
                def two(t):
                    first(t + 1, 1)
                    second(t, 0)
                    first(t + 2, 0)
                    second(t + 1, 1)

                first(0, 0)
                two(0)
                with pe.Fori(2, NT - 3, 2) as t:
                    two(t)
                first(NT - 1, 1)
                second(NT - 2, 0)
                second(NT - 1, 1)

            def oproj_t(t, p):
                pe.wait_ge(nn, t + 1)
                if not isinstance(t, int) or t >= 2:
                    pe.wait_ge(ot_ready, t - 1)
                nc.tensor.transpose(bank[p][:, 0:TT], xn[:, p, 0:P], ident[0:TT, 0:TT])
                nc.tensor.transpose(bank[p][0:D1, P:P + TT], xn[:, p, P:DIM], ident[0:TT, 0:TT]).then_inc(ot_done, 1)

            pair(oproj_t, oproj)

            def n_t(t, p):
                pe.wait_ge(yn, t + 1)
                if not isinstance(t, int) or t >= 2:
                    pe.wait_ge(nt_ready, t - 1)
                nc.tensor.transpose(bank[p][:, 0:TT], xn[:, p, 0:P], ident[0:TT, 0:TT])
                nc.tensor.transpose(bank[p][0:D1, P:P + TT], xn[:, p, P:DIM], ident[0:TT, 0:TT]).then_inc(nt_done, 1)

            def n_g(t, p):
                pe.wait_ge(nt_ready, t + 1)
                if not isinstance(t, int) or t >= 2:
                    pe.wait_ge(logits_in, t - 1)
                nc.tensor.matmul(bank[2 + p][0:TT, 0:EXPERTS], xt_a[:, p, :], gatew[:, 0, :], start=True, stop=False)
                nc.tensor.matmul(bank[2 + p][0:TT, 0:EXPERTS], xt_b[0:D1, p, :], gatew[0:D1, 1, :],
                                 start=False, stop=True).then_inc(g_done, 1)

            pair(n_t, n_g)

            pe.wait_ge(tri_loaded, 16)
            pe.wait_ge(oh_ready, 1)
            for i in range(2):
                last = nc.tensor.matmul(bank[i][0:TT, 0:NT * EXPERTS], tri[:, i, :],
                                        oh[:, :, :].rearrange("p t e -> p (t e)"), start=True, stop=True)
            last.then_inc(ranked, 1)

            def ps_h(p):
                return psum[:, 3 * p:3 * p + 3, :].rearrange("p b n -> p (b n)")

            ps_t = psum[:, 6, :].bitcast(f16)
            ps_y = psum[:, 7, :]

            def slot_t(s_, p):
                pe.wait_ge(xs_in[p], 8 * (s_ - p) + 16)
                if not isinstance(s_, int) or s_ >= 1:
                    pe.wait_ge(xe, s_)
                for j in range(SUB):
                    x16 = xs[p][:, j, 0:DIM].bitcast(f16)
                    for i in range(3):
                        n = (j * 3 + i) * P
                        last = nc.tensor.transpose(ps_t[:, n:n + P], x16[:, i * P:(i + 1) * P], identh[:, :])
                last.then_inc(tt_done, 1)

            def slot_h(s_, p, w1o):
                pe.wait_ge(xe, s_ + 1)
                if not isinstance(s_, int) or s_ >= 2:
                    pe.wait_ge(gelu, s_ - 1)
                hi_a, hl_b, lo_a = (xt16[:, p, i, :] for i in range(3))
                for c in range(HC):
                    o = ps_h(p)[:, c * ST:(c + 1) * ST]
                    terms = ((w1ah, hi_a, P), (w1ah, lo_a, P), (w1al, hi_a, P), (w1bh, hl_b, P),
                             (w1bl, xl16[:, p, :], D1 + 2))
                    for n, (w, xx, k) in enumerate(terms):
                        last = nc.tensor.matmul(o, w[0:k, bass.ds(w1o + c * P, P)], xx,
                                                start=(n == 0), stop=(n == len(terms) - 1))
                last.then_inc(h_done, 1)

            def slot_y(s_, p, w2o, b2o):
                pe.wait_ge(split, s_ + 1)
                if not isinstance(s_, int) or s_ >= 1:
                    pe.wait_ge(y_ev, s_)
                for c in range(HC):
                    for a, w in ((hh[p], w2h), (hl[p], w2h), (hh[p], w2l)):
                        for j in range(SUB):
                            n = c * ST + j * P
                            nc.tensor.matmul(ps_y[:, j * DIM:(j + 1) * DIM], a[:, n:n + P],
                                             w[:, bass.ds(w2o + c * DIM, DIM)],
                                             start=(c == 0 and j == 0 and a is hh[p] and w is w2h), stop=False,
                                             skip_group_check=True)
                for j in range(SUB):
                    last = nc.tensor.matmul(ps_y[:, j * DIM:(j + 1) * DIM], ones16[:, :], b2hl[:, bass.ds(b2o, DIM)],
                                            start=False, stop=True, skip_group_check=True)
                last.then_inc(y_done, 1)

            def expert(s_):
                return pe.value_load(etab[0:1, bass.ds(s_, 1)], min_val=0, max_val=EXPERTS - 1)

            def h_step(s_, p):
                slot_h(s_, p, pe.snap(expert(s_) * HID))

            def y_step(s_, p):
                e = expert(s_)
                slot_y(s_, p, pe.snap(e * (HC * DIM)), pe.snap(e * DIM))

            pe.wait_ge(routed, 1)
            slot_t(0, 0)
            for s_ in range(2):
                slot_t(s_ + 1, 1 - s_)
                h_step(s_, s_)
            def both(s_, p):
                slot_t(s_ + 1, 1 - p)
                h_step(s_, p)
                y_step(s_ - 2, p)

            both(2, 0)
            both(3, 1)
            with pe.Fori(4, NS - 3, 2) as s_:
                both(s_, 0)
                both(s_ + 1, 1)
            slot_t(NS - 1, 1)
            h_step(NS - 2, 0)
            y_step(NS - 4, 0)
            h_step(NS - 1, 1)
            y_step(NS - 3, 1)
            y_step(NS - 2, 0)
            y_step(NS - 1, 1)

        @block.vector
        def _(dve):
            V = nc.vector

            def emb_add(t, j):
                dve.wait_ge(em_done, t + 1)
                V.tensor_tensor(h[:, bass.ds(t, 1), :].rearrange("p a d -> p (a d)"),
                                allbanks[6 + j][0:TT, 0:DIM], posb, ALU.add).then_inc(ea_done, 1)
                tile_stats(h, t, j, 0, ea_done)

            def alone(s_, value):
                value = value if isinstance(value, int) else dve.to_reg(value)
                dve.wait_ge(zeroed, 3)
                dve.wait_ge(s_, value)

            def halves_stats(src, t, p, which, written):
                alone(written, t + 1)
                V.bn_stats(stats[:, which, p, :],
                           src[:, bass.ds(t, 1), :].rearrange("p a d -> p (a d)")).then_inc(stat[which], 1)

            def aggregate(t, p, which):
                if which != 2 and (not isinstance(t, int) or t >= 2):
                    alone(rstd_in[which], t - 1)
                alone(stat[which], t + 1)
                V.bn_aggr(meanvar[:, which, p, :], stats[:, which, p, :]).then_inc(aggr[which], 1)

            def tile_stats(src, t, p, which, written):
                halves_stats(src, t, p, which, written)
                aggregate(t, p, which)

            def normalise(src, t, p, which, done):
                dve.wait_ge(rstd_in[which], t + 1)
                V.tensor_scalar(xn[:, p, :], src[:, bass.ds(t, 1), :].rearrange("p a d -> p (a d)"),
                                mean[:, which, bass.ds(t, 1)],
                                rstd[:, which, bass.ds(t, 1)], ALU.subtract, ALU.mult).then_inc(done, 1)

            V.memset(qxbuf[:, :], 0.0).then_inc(zeroed, 1)
            V.memset(mx[:, :], 0.0).then_inc(zeroed, 1)
            V.memset(w1ah[:, 0:2 * XW], 0.0).then_inc(zeroed, 1)
            V.memset(ones16[:, :], 1.0).then_inc(ones_set, 1)
            V.memset(xl16[D1:D1 + 2, :, :], XS).then_inc(ones_set, 1)
            dve.wait_ge(zeroed, 3)
            dve.wait_ge(consts, CONSTS)
            V.tensor_tensor(posb, posb, bias_cls, ALU.add).then_inc(posb_ready, 1)
            V.tensor_copy(identh[:, :], ident[:, :]).then_inc(posb_ready, 1)
            dve.wait_ge(posb_ready, 2)
            emb_add(0, 0)
            emb_add(1, 1)
            with dve.Fori(2, NT - 1, 2) as t:
                emb_add(t, 0)
                emb_add(t + 1, 1)

            dve.wait_ge(late_in, 16 * 3)

            def low_w1(e):
                dve.wait_ge(w_high, 2 * e + 1)
                V.scalar_tensor_tensor(out=w1al[:, bass.ds(e * HID, HID)], in0=st_a, scalar=W1S,
                                       in1=w1ah[:, bass.ds(e * HID, HID)], op0=ALU.mult, op1=ALU.subtract)

            def low_w2(e):
                dve.wait_ge(w_high, 2 * e + 2)
                V.scalar_tensor_tensor(out=w2l[:, bass.ds(e * (HC * DIM), HC * DIM)], in0=st_w2, scalar=W2S,
                                       in1=w2h[:, bass.ds(e * (HC * DIM), HC * DIM)], op0=ALU.mult,
                                       op1=ALU.subtract)

            def low_bias(e):
                V.scalar_tensor_tensor(out=w1bl[:, bass.ds(e * HID, HID)], in0=st_l[0:D1 + 2], scalar=W1S,
                                       in1=tmp_l[:, :], op0=ALU.mult, op1=ALU.subtract)
                V.scalar_tensor_tensor(out=b2hl[:, bass.ds(e * DIM, DIM)], in0=st_b2, scalar=W2S,
                                       in1=tmp_b2[:, :], op0=ALU.mult, op1=ALU.subtract).then_inc(w_low, 1)

            for l in range(2):
                s = L[l]
                src, which = (h, 0) if l == 0 else (xall, 2)

                def block_in(t, p):
                    dve.wait_ge(rstd_in[1], t + 1)
                    V.tensor_scalar(xall[:, bass.ds(t, 1), :].rearrange("p a d -> p (a d)"),
                                    h[:, bass.ds(t, 1), :].rearrange("p a d -> p (a d)"),
                                    mean[:, 1, bass.ds(t, 1)],
                                    rstd[:, 1, bass.ds(t, 1)], ALU.subtract, ALU.mult).then_inc(x0, 1)
                    tile_stats(xall, t, p, 2, x0)

                def ln(t, p):
                    normalise(src, t, p, which, s["xn"])

                def xt_ev(t, p, l=l, s=s):
                    dve.wait_ge(s["t_done"], t + 1)
                    if l == 0:
                        V.tensor_copy(xt_a[:, p, :], v_ps[:, 256:256 + TT])
                        V.tensor_copy(xt_b[0:D1, p, :], v_ps[0:D1, 384:384 + TT]).then_inc(s["xt"], 1)
                    else:
                        V.tensor_scalar(xt_a[:, p, :], v_ps[:, 256:256 + TT], lnw[:, 0:1], lnw[:, 1:2],
                                        ALU.mult, ALU.add)
                        V.tensor_scalar(xt_b[0:D1, p, :], v_ps[0:D1, 384:384 + TT], lnw[0:D1, 2:3],
                                        lnw[0:D1, 3:4], ALU.mult, ALU.add).then_inc(s["xt"], 1)

                def k_ev(t, p):
                    dve.wait_ge(s["k_done"], t + 1)
                    V.tensor_copy(kt[:, p, :, :].rearrange("p m t -> p (m t)"),
                                  k_ps[:, 0:MT * TT]).then_inc(s["k_ready"], 1)

                def m_ev(t, p):
                    dve.wait_ge(s["mt_done"], t + 1)
                    for i in range(SH // 2, SH):
                        last = V.tensor_copy(qx[i * SLOT:i * SLOT + MT, p, :, i, :], maxima(i))
                    last.then_inc(s["m_ready2"], 1)

                def v_ev(t, p):
                    dve.wait_ge(s["v_high"], t + 1)
                    v = v_ps[0:TT, 0:HEADS * VW].rearrange("p (h d) -> p h d", d=VW)
                    V.scalar_tensor_tensor(out=vt[:, p, :, VW:2 * VW], in0=v, scalar=XS, in1=vt[:, p, :, 0:VW],
                                           op0=ALU.mult, op1=ALU.subtract).then_inc(s["v_ready"], 1)

                def maxes(t):
                    for m in range(MT):
                        dve.wait_ge(s["s_done"], 3 * t + m + 1)
                        last = V.tensor_reduce(
                            mx[:, :].rearrange("p (i c) -> p i c", c=SLOT)[:, :, m:m + 1],
                            s_ps[0:TT, m, 0:SH * TT].rearrange("p (i t) -> p i t", t=TT), AX, ALU.max, negate=True)
                    last.then_inc(s["max"], 1)

                def take(t):
                    dve.wait_ge(s["part"], t + 1)
                    o = o_ps[0:TT, 0:HEADS * 2 * VW].rearrange("p (h d) -> p h d", d=2 * VW)
                    V.tensor_tensor(osum[:, :, :], o[:, :, 0:VW], osum[:, :, :], ALU.add).then_inc(s["osum"], 1)
                    dve.wait_ge(s["osum"], t + 1)
                    V.reciprocal(rs[:, :], osum[:, :, HD:VW].rearrange("p h a -> p (h a)")).then_inc(s["rec"], 1)
                    dve.wait_ge(s["rec"], t + 1)
                    tile = (onorm[:, :] if l == 0 else
                            oall[:, bass.ds(t, 1), :].rearrange("p a d -> p (a d)"))
                    V.tensor_tensor(tile.rearrange("p (h d) -> p h d", d=HD), osum[:, :, 0:HD],
                                    rs[:, :].rearrange("p (h a) -> p h a", a=1).to_broadcast([TT, HEADS, HD]),
                                    ALU.mult).then_inc(s["norm"], 1)

                def residual(t, p):
                    if l == 0:
                        dve.wait_ge(s["norm"], t + 1)
                        ht_ = h[:, bass.ds(t, 1), :].rearrange("p a d -> p (a d)")
                        V.tensor_tensor(ht_, ht_, onorm[:, :], ALU.add).then_inc(h_in, 1)
                        tile_stats(h, t, p, 1, h_in)

                def start(t, p):
                    maxes(t)
                    if inside(t, 1):
                        k_ev(t + 1, 1 - p)
                    m_ev(t, p)

                def finish(t, p):
                    if inside(t, 1):
                        v_ev(t + 1, 1 - p)
                    if l == 0 and (not isinstance(t, int) or t >= 2):
                        block_in(t - 2, p)
                    if inside(t, -1):
                        take(t - 1)
                    if inside(t, 2):
                        xt_ev(t + 2, p)
                    if inside(t, -1):
                        residual(t - 1, 1 - p)
                    if inside(t, 3):
                        ln(t + 3, 1 - p)

                def step(t, p):
                    start(t, p)
                    finish(t, p)

                if l == 0:
                    ln(0, 0)
                    ln(1, 1)
                    xt_ev(0, 0)
                ln(2, 0)
                if l == 1:
                    block_in(NT - 2, 0)
                k_ev(0, 0)
                v_ev(0, 0)
                xt_ev(1, 1)
                if l == 1:
                    block_in(NT - 1, 1)
                step(0, 0)
                for t in range(1, 3):
                    step(t, t % 2)
                with dve.Fori(0, LE) as e:
                    step(4 * e + 3, 1)
                    start(4 * e + 4, 0)
                    low_w1(e + l * LE)
                    finish(4 * e + 4, 0)
                    start(4 * e + 5, 1)
                    low_w2(e + l * LE)
                    finish(4 * e + 5, 1)
                    start(4 * e + 6, 0)
                    low_bias(e + l * LE)
                    finish(4 * e + 6, 0)
                for t in range(4 * LE + 3, NT):
                    step(t, t % 2)
                if l == 0:
                    for t in range(2):
                        normalise(xall, t, t, 2, L[1]["xn"])
                    xt_ev(0, 0, 1, L[1])
                take(NT - 1)
                residual(NT - 1, 1)

            def o_add(t, p):
                dve.wait_ge(pj_done, t + 1)
                xs = xall[:, bass.ds(t, 1), :].rearrange("p a d -> p (a d)")
                V.tensor_tensor(xs, bank[2 + p][0:TT, 0:DIM], xs, ALU.add).then_inc(x2, 1)
                if not isinstance(t, int) or t >= 1:
                    aggregate(t - 1, 1 - p, 3)
                halves_stats(xall, t, p, 3, x2)

            for t in range(4):
                o_add(t, t % 2)
            with dve.Fori(4, NT - 1, 2) as t:
                o_add(t, 0)
                o_add(t + 1, 1)
            aggregate(NT - 1, 1, 3)

            dve.wait_ge(ot_done, NT)
            dve.wait_ge(ln2_scaled, 1)

            def n_ln(t, p):
                if not isinstance(t, int) or t >= 2:
                    dve.wait_ge(nt_done, t - 1)
                    dve.wait_ge(row_split, t - 1)
                normalise(xall, t, p, 3, ync)
                for i, op in enumerate((ALU.mult, ALU.add)):
                    dve.wait_ge(ync, 2 * t + i + 1)
                    V.tensor_tensor(xn[:, p, :], xn[:, p, :], ln2w[:, i, :], op).then_inc((ync, yn)[i], 1)

            def n_gate(t, p):
                dve.wait_ge(g_done, t + 1)
                V.tensor_scalar(logits[:, bass.ds(t, 1), :].rearrange("p a e -> p (a e)"),
                                bank[2 + p][0:TT, 0:EXPERTS], 1.0 / XS, None, ALU.mult).then_inc(logits_in, 1)

            for t in range(2):
                n_ln(t, t)
            with dve.Fori(2, NT - 1, 2) as t:
                for p in range(2):
                    n_ln(t + p, p)
                    n_gate(t + p - 2, p)
            for t in range(NT - 2, NT):
                n_gate(t, t % 2)

            chained = [0]

            def link(ins):
                ins.then_inc(gchain, 1)
                chained[0] += 1
                dve.wait_ge(gchain, chained[0])

            def wide(a):
                return a.rearrange("p (t a) -> p t a", a=1).to_broadcast([TT, NT, EXPERTS])

            def find(onehot, top_):
                link(V.tensor_reduce(top_, logits[:, :, :], AX, ALU.max))
                link(V.tensor_tensor(onehot, logits[:, :, :], wide(top_), ALU.is_equal))
                link(V.tensor_scalar(onehot, onehot, -float(EXPERTS), float(EXPERTS), ALU.mult, ALU.add))
                link(V.tensor_tensor(onehot, onehot, rc("iota"), ALU.add))
                link(V.tensor_reduce(gm[:, 3, :], onehot, AX, ALU.min))
                link(V.tensor_tensor(onehot, rc("iota"), wide(gm[:, 3, :]), ALU.is_equal))

            dve.wait_ge(logits_in, NT)
            find(first[:, :, :], gm[:, 0, :])
            link(V.tensor_scalar(second[:, :, :], first[:, :, :], -1.0, 1.0, ALU.mult, ALU.add))
            link(V.tensor_tensor(logits[:, :, :], logits[:, :, :], second[:, :, :], ALU.mult))
            link(V.tensor_scalar(second[:, :, :], first[:, :, :], -3.0e38, None, ALU.mult))
            link(V.tensor_tensor(logits[:, :, :], logits[:, :, :], second[:, :, :], ALU.add))
            find(second[:, :, :], gm[:, 1, :])
            valid = rc("valid").rearrange("p a t -> p (a t)")
            for one_hot in (first, second):
                link(V.tensor_tensor(one_hot[:, :, :], one_hot[:, :, :], wide(valid), ALU.mult))
            V.tensor_tensor(oh[:, :, :], first[:, :, :], second[:, :, :], ALU.add).then_inc(oh_ready, 1)
            V.tensor_tensor(gm[:, 1, :], gm[:, 1, :], gm[:, 0, :], ALU.subtract).then_inc(gdiff, 1)
            dve.wait_ge(gexp, 1)
            link(V.tensor_scalar(gm[:, 0, :], gm[:, 1, :], 1.0, W2S, ALU.add, ALU.mult))
            link(V.reciprocal(gm[:, 0, :], gm[:, 0, :]))
            link(V.tensor_tensor(gm[:, 1, :], gm[:, 1, :], gm[:, 0, :], ALU.mult))
            for i, rows in enumerate((rows0, rows1)):
                V.tensor_copy(rows[:, :, DIM:DIM + 1].rearrange("p t a -> p (t a)"), gm[:, i, :])
                V.tensor_copy(rows[:, :, DIM + 1:XW].rearrange("p t a -> p (t a)"), rc("dest")[:, i, :])

            tiles, before, through, start = (small[:, i, :] for i in range(4))
            dve.wait_ge(ranked, 1)
            flat = "p t e -> p (t e)"
            link(V.tensor_copy(cnt[:, :, :].rearrange(flat), bank[1][0:TT, 0:NT * EXPERTS]))
            for e in range(EXPERTS):
                last = V.tensor_tensor_scan(place[:, :, e:e + 1].rearrange("p t a -> p (t a)"),
                                            rc("ones").rearrange("p a t -> p (a t)"),
                                            cnt[:, :, e:e + 1].rearrange("p t a -> p (t a)"), 0.0,
                                            ALU.mult, ALU.add)
            link(last)

            def down(a, n):
                return a.rearrange("p (e a) -> p e a", a=1).to_broadcast([TT, EXPERTS, n])

            def across(a, rows, n):
                return a.rearrange("p (a e) -> p a e", a=1).to_broadcast([rows, n, EXPERTS])

            filled = logits[:, :, :].rearrange(flat)[:, 0:EXPERTS * MAXT].rearrange("p (e k) -> p e k", k=MAXT)
            link(V.tensor_copy(start, place[:, NT - 1, :]))
            link(V.tensor_tensor(filled, down(start, MAXT), rc("thr"), ALU.is_gt))
            link(V.tensor_reduce(tiles, filled, AX, ALU.add))
            lower = logits[:, 0:EXPERTS, :]
            link(V.tensor_tensor(lower, across(tiles, TT, EXPERTS), rc("tri8"), ALU.mult))
            link(V.tensor_reduce(before, lower, AX, ALU.add))
            link(V.tensor_tensor(through, before, tiles, ALU.add))
            link(V.tensor_scalar(start, before, float(ST), None, ALU.mult))
            link(V.tensor_tensor(place[:, :, :], place[:, :, :], cnt[:, :, :], ALU.subtract))
            link(V.tensor_tensor(place[:, :, :].rearrange(flat), bank[0][0:TT, 0:NT * EXPERTS],
                                 place[:, :, :].rearrange(flat), ALU.add))
            link(V.tensor_tensor(place[:, :, :], place[:, :, :], across(start, TT, NT), ALU.add))
            for i, one_hot in enumerate((first, second)):
                link(V.tensor_tensor(one_hot[:, :, :], one_hot[:, :, :], place[:, :, :], ALU.mult))
                link(V.tensor_reduce(gm[:, 2 + i, :], one_hot[:, :, :], AX, ALU.add))
                link(V.tensor_tensor(pos_i[:, i, :], gm[:, 2 + i, :], rc("outside").rearrange("p a t -> p (a t)"),
                                     ALU.add))
            past = etf[:, :, :]
            link(V.tensor_tensor(past, rc("tile", 1), across(through[0:1], 1, NS), ALU.is_ge))
            link(V.tensor_reduce(etn[:, :], past, AX, ALU.add))
            V.tensor_scalar(etab[:, :], etn[:, :], float(EXPERTS - 1), None, ALU.min).then_inc(routed, 1)

            def split_h(s_, p):
                dve.wait_ge(gelu, s_ + 1)
                if not isinstance(s_, int) or s_ >= 2:
                    dve.wait_ge(y_done, s_ - 1)
                V.tensor_copy(hh[p], h32).then_inc(hi_done, 1)
                dve.wait_ge(hi_done, s_ + 1)
                V.tensor_tensor(hl[p], h32, hh[p], ALU.subtract).then_inc(split, 1)

            def gate_y(s_, p):
                dve.wait_ge(y_done, s_ + 1)
                dve.wait_ge(fields_in, s_ + 1)
                if not isinstance(s_, int) or s_ >= 2:
                    dve.wait_ge(y_out[p], 8 * SUB * (s_ - p))
                V.tensor_scalar(dest[:, p, :], fields[:, bass.ds(s_, 1), :, 1:2].rearrange("p s j a -> p (s j a)"),
                                float(OUTSIDE), None, ALU.add)
                for j in range(SUB):
                    last = V.tensor_scalar(yg[:, p, j, :], psum[:, 7, j * DIM:(j + 1) * DIM],
                                           fields[:, bass.ds(s_, 1), j, 0:1].rearrange("p s a -> p (s a)"),
                                           None, ALU.mult)
                last.then_inc(y_ev, 1)

            split_h(0, 0)
            split_h(1, 1)
            gate_y(0, 0)
            split_h(2, 0)
            gate_y(1, 1)
            split_h(3, 1)
            with dve.Fori(2, NS - 3, 2) as s_:
                for p in range(2):
                    gate_y(s_ + p, p)
                    split_h(s_ + p + 2, p)
            gate_y(NS - 2, 0)
            gate_y(NS - 1, 1)

            dve.wait_ge(resd, NT)
            for n, (t0, k, r) in enumerate(CHUNKS):
                dve.wait_ge(back[n], 32)
                V.tensor_tensor(h[0:r, t0:t0 + k, :], h[0:r, t0:t0 + k, :], xall[0:r, t0:t0 + k, :],
                                ALU.add).then_inc(summed, 1)
                dve.wait_ge(summed, n + 1)
                V.tensor_tensor(h[0:r, t0:t0 + k, :], h[0:r, t0:t0 + k, :], oall[0:r, t0:t0 + k, :],
                                ALU.add).then_inc(added, 1)

        @block.scalar
        def _(act):
            A = nc.scalar

            act.wait_ge(zeroed, 3)

            def high_w1(e):
                act.wait_ge(w_in, 16 * PREP * (e + 1))
                act.wait_ge(cleared, 16)
                A.activation(w1ah[:, bass.ds(e * HID, HID)], st_a, ACT.Copy, scale=W1S)
                A.activation(w1bh[:, bass.ds(e * HID, HID)], st_b, ACT.Copy, scale=W1S).then_inc(w_high, 1)

            def high_rest(e):
                act.wait_ge(w_low, e)
                A.activation(w2h[:, bass.ds(e * (HC * DIM), HC * DIM)], st_w2, ACT.Copy, scale=W2S)
                A.activation(tmp_l[:, :], st_l[0:D1 + 2], ACT.Identity, scale=keep_low[0:D1 + 2, 0:1])
                A.activation(tmp_b2[:, :], st_b2, ACT.Identity, scale=keep_low[0:2, 1:2]).then_inc(w_high, 1)

            def o_cp(t, p):
                act.wait_ge(L[1]["norm"], t + 1)
                A.copy(xn[:, p, :], oall[:, bass.ds(t, 1), :].rearrange("p a d -> p (a d)")).then_inc(nn, 1)

            for l in range(2):
                s = L[l]

                def q_ev(t, p):
                    act.wait_ge(s["q_done"], t + 1)
                    for i in range(SH):
                        last = A.copy(qx[i * SLOT:(i + 1) * SLOT, p, :, i, :],
                                      q_ps[i * SLOT:(i + 1) * SLOT, 0:MT * TT].rearrange("p (m t) -> p m t", t=TT))
                    last.then_inc(s["q_ready"], 1)

                def m_ev(t, p):
                    act.wait_ge(s["mt_done"], t + 1)
                    for i in range(SH // 2):
                        last = A.copy(qx[i * SLOT:i * SLOT + MT, p, :, i, :], maxima(i))
                    last.then_inc(s["m_ready"], 1)

                def v_ev(t, p):
                    act.wait_ge(s["v_done"], t + 1)
                    if not isinstance(t, int) or t >= 2:
                        act.wait_ge(s["av"], t - 1)
                    A.activation(vt[:, p, :, 0:VW], v_ps[0:TT, 0:HEADS * VW].rearrange("p (h d) -> p h d", d=VW),
                                 ACT.Copy, scale=XS).then_inc(s["v_high"], 1)

                def part(t):
                    act.wait_ge(s["av"], t + 1)
                    if not isinstance(t, int) or t >= 1:
                        act.wait_ge(s["norm"], t)
                    A.copy(osum[:, :, :], o_ps[0:TT, 0:HEADS * 2 * VW].rearrange(
                        "p (h d) -> p h d", d=2 * VW)[:, :, VW:2 * VW]).then_inc(s["part"], 1)

                def exps(t):
                    for m in range(MT):
                        act.wait_ge(s["st_done"], 3 * t + m + 1)
                        if not isinstance(t, int) or t >= 1:
                            act.wait_ge(s["low"], 3 * t - 2 + m)
                        A.activation(pt32[:, m, :], s_ps[0:TT, m, 0:SH * TT], ACT.Exp, scale=HD ** -0.5)
                        A.activation(pt_high[:, m * SH:(m + 1) * SH, :].rearrange("p h t -> p (h t)"),
                                     s_ps[0:TT, m, 0:SH * TT], ACT.Exp, scale=HD ** -0.5).then_inc(s["exp"], 1)

                def step(t, p):
                    if inside(t, 1):
                        q_ev(t + 1, 1 - p)
                    m_ev(t, p)
                    if inside(t, 1):
                        v_ev(t + 1, 1 - p)
                    if inside(t, -1):
                        part(t - 1)
                    exps(t)

                q_ev(0, 0)
                v_ev(0, 0)
                step(0, 0)
                for t in range(1, 3):
                    step(t, t % 2)
                with act.Fori(0, LE) as e:
                    step(4 * e + 3, 1)
                    high_w1(e + l * LE)
                    step(4 * e + 4, 0)
                    high_rest(e + l * LE)
                    step(4 * e + 5, 1)
                    step(4 * e + 6, 0)
                for t in range(4 * LE + 3, NT):
                    step(t, t % 2)
                if l == 1:
                    act.wait_ge(s["t_done"], NT)
                    for t in range(2):
                        o_cp(t, t)
                part(NT - 1)

            act.wait_ge(L[1]["norm"], NT)

            def transposed(t, p, done, used, ready):
                act.wait_ge(done, t + 1)
                if not isinstance(t, int) or t >= 2:
                    act.wait_ge(used, t - 1)
                A.copy(xt_a[:, p, :], bank[p][:, 0:TT])
                A.copy(xt_b[0:D1, p, :], bank[p][0:D1, P:P + TT]).then_inc(ready, 1)

            def o_ev(t, p):
                transposed(t, p, ot_done, pj_done, ot_ready)

            for t in range(2):
                o_ev(t, t)
                o_cp(t + 2, t)
            with act.Fori(2, NT - 3, 2) as t:
                for p in range(2):
                    o_ev(t + p, p)
                    o_cp(t + p + 2, p)
            for t in range(NT - 2, NT):
                o_ev(t, t % 2)

            act.wait_ge(pj_done, NT)
            act.wait_ge(resd, NT)

            def n_high(t, p):
                act.wait_ge(yn, t + 1)
                for r in (rows16, rows16_1):
                    last = A.copy(r[:, bass.ds(t, 1), 0:DIM].rearrange("p a n -> p (a n)"), xn[:, p, :])
                last.then_inc(row_high, 1)

            def n_ev(t, p):
                n_high(t, p)
                transposed(t, p, nt_done, g_done, nt_ready)

            for t in range(2):
                n_ev(t, t)
            with act.Fori(2, NT - 1, 2) as t:
                n_ev(t, 0)
                n_ev(t + 1, 1)

            act.wait_ge(gdiff, 1)
            A.activation(gm[:, 1, :], gm[:, 1, :], ACT.Exp).then_inc(gexp, 1)

            def slot_ev(s_, p):
                act.wait_ge(tt_done, s_ + 1)
                if not isinstance(s_, int) or s_ >= 2:
                    act.wait_ge(h_done, s_ - 1)
                src = psum[:, 6, :].bitcast(f16)[:, 0:3 * ST].rearrange("p (j i n) -> p i j n", j=SUB, i=3)
                A.copy(xt16[:, p, :, :].rearrange("p i (j n) -> p i j n", j=SUB), src)
                A.copy(xl16[0:D1, p, :].rearrange("p (j n) -> p j n", j=SUB), src[0:D1, 1]).then_inc(xe, 1)

            def hidden(s_, p):
                act.wait_ge(h_done, s_ + 1)
                if not isinstance(s_, int) or s_ >= 1:
                    act.wait_ge(split, s_)
                A.activation(h32, psum[:, 3 * p:3 * p + 3, :].rearrange("p b n -> p (b n)"), ACT.Gelu,
                             scale=1.0 / (XS * W1S)).then_inc(gelu, 1)

            slot_ev(0, 0)
            slot_ev(1, 1)
            hidden(0, 0)
            slot_ev(2, 0)
            hidden(1, 1)
            slot_ev(3, 1)
            with act.Fori(2, NS - 3, 2) as s_:
                for p in range(2):
                    hidden(s_ + p, p)
                    slot_ev(s_ + p + 2, p)
            hidden(NS - 2, 0)
            hidden(NS - 1, 1)

        @block.gpsimd
        def _(pool):
            pool.memset(half[:, :], -0.5).then_inc(half_set, 1)
            pool.wait_ge(half_set, 1)
            def alone(s_, value):
                value = value if isinstance(value, int) else pool.to_reg(value)
                pool.wait_ge(half_set, 1)
                pool.wait_ge(s_, value)


            def deviation(which, t, p):
                alone(aggr[which], t + 1)
                pool.tensor_scalar(vareps[:, which, p:p + 1], meanvar[:, which, p, 1:2], EPS, None,
                                   ALU.add).then_inc(eps_in[which], 1)
                pool.tensor_copy(mean[:, which, bass.ds(t, 1)], meanvar[:, which, p, 0:1])
                alone(eps_in[which], t + 1)
                pool.tensor_tensor(rstd[:, which, bass.ds(t, 1)], vareps[:, which, p:p + 1], half[:, :],
                                   ALU.pow).then_inc(rstd_in[which], 1)

            def low(l, t):
                for m in range(MT):
                    alone(L[l]["exp"], 3 * t + m + 1)
                    pool.tensor_tensor(pt_low[:, m * SH:(m + 1) * SH, :].rearrange("p h t -> p (h t)"), pt32[:, m, :],
                                       pt_high[:, m * SH:(m + 1) * SH, :].rearrange("p h t -> p (h t)"),
                                       ALU.subtract).then_inc(L[l]["low"], 1)

            def first_layer(t, p):
                deviation(2, t - 2, p)
                deviation(1, t - 1, 1 - p)
                low(0, t)

            with pool.Fori(0, NT - 1, 2) as t:
                deviation(0, t, 0)
                deviation(0, t + 1, 1)
            low(0, 0)
            deviation(1, 0, 0)
            low(0, 1)
            with pool.Fori(2, NT - 1, 2) as t:
                first_layer(t, 0)
                first_layer(t + 1, 1)
            deviation(2, NT - 2, 0)
            deviation(1, NT - 1, 1)
            deviation(2, NT - 1, 1)
            with pool.Fori(0, NT) as t:
                low(1, t)
            pool.wait_ge(end_in, 16 * 5)
            pool.tensor_scalar(ln2w, ln2w, XS, None, ALU.mult).then_inc(ln2_scaled, 1)

            def residual(t):
                alone(x2, t + 1)
                hs, xs = (v[:, bass.ds(t, 1), :].rearrange("p a d -> p (a d)") for v in (h, xall))
                pool.tensor_tensor(hs, hs, xs, ALU.add).then_inc(resd, 1)

            with pool.Fori(0, NT - 1, 2) as t:
                for p in range(2):
                    deviation(3, t + p, p)
                    residual(t + p)

            def n_low(t, p):
                alone(row_high, t + 1)
                r = rows16[:, bass.ds(t, 1), :].rearrange("p a n -> p (a n)")
                pool.tensor_tensor(r[:, DIM:DIM + D1], xn[:, p, P:DIM], r[:, P:DIM], ALU.subtract)
                pool.tensor_tensor(r[:, DIM + D1:2 * DIM], xn[:, p, 0:P], r[:, 0:P],
                                   ALU.subtract).then_inc(row_split, 1)

            def copy_row(t):
                alone(row_split, t + 1)
                pool.tensor_copy(rows1[:, bass.ds(t, 1), DIM // 2:DIM].rearrange("p a n -> p (a n)"),
                                 rows0[:, bass.ds(t, 1), DIM // 2:DIM].rearrange("p a n -> p (a n)")
                                 ).then_inc(row_copied, 1)

            with pool.Fori(0, NT - 1, 2) as t:
                for p in range(2):
                    n_low(t + p, p)
                    copy_row(t + p)

            pool.wait_ge(routed, 1)
            pool.wait_ge(cleared, 16)
            pool.wait_ge(row_copied, NT)
            for t in range(NT):
                for i, rows in enumerate((rows0, rows1)):
                    pool.indirect_dma_start(slots, bass.IndirectOffsetOnAxis(ap=pos_i[:, i, t:t + 1], axis=0),
                                            rows[:, t, :], None, bounds_check=NSLOT - 1,
                                            oob_is_err=False).then_inc(scattered, 16)

            def take_fields(s_, p):
                alone(xs_in[p], 8 * (s_ - p) + 16)
                pool.tensor_copy(fields[:, bass.ds(s_, 1), :, :].rearrange("p s j a -> p (s j) a"),
                                 xs[p][:, :, DIM:XW]).then_inc(fields_in, 1)

            def scatter_y(s_, p):
                alone(y_ev, s_ + 1)
                for j in range(SUB):
                    pool.indirect_dma_start(ymoe, bass.IndirectOffsetOnAxis(ap=dest[:, p, j:j + 1], axis=0),
                                            yg[:, p, j, :], None, bounds_check=last_row,
                                            oob_is_err=False).then_inc(y_out[p], 16)

            last_row = pool.to_reg(2 * NT * TT - 1)
            for s_ in range(AHEAD):
                take_fields(s_, s_ % 2)
            for s_ in range(2):
                take_fields(s_ + AHEAD, s_ % 2)
                scatter_y(s_, s_ % 2)
            with pool.Fori(2, NS - AHEAD - 1, 2) as s_:
                for p in range(2):
                    take_fields(s_ + p + AHEAD, p)
                    scatter_y(s_ + p, p)
            for s_ in range(NS - AHEAD, NS):
                scatter_y(s_, s_ % 2)


def _slots(wa, ba, wb, bb):
    head = MT + TI
    w = np.zeros((DIM + 4, 2, MT, SH, SLOT), np.float32)
    for n, (wm, bm) in enumerate(((wa, ba), (wb, bb))):
        w[:DIM, n, :, :, head:head + HD] = wm.reshape(DIM, MT, SH, HD)
        w[DIM, n, :, :, head:head + HD] = bm.reshape(MT, SH, HD)
    for m in range(MT):
        w[DIM, 1, m, :, m] = 1.0
    for i in range(TI):
        w[DIM + 1 + i, 0, :, :, MT + i] = 1.0
        w[DIM, 1, :, :, MT + i] = -BIG
        w[DIM + 1 + i, 1, :, :, MT + i] = BIG
    return w.reshape(DIM + 4, 2 * MT * P)


def _values(wm, bm):
    w = np.zeros((DIM + 4, HEADS, VW), np.float32)
    w[:DIM, :, :HD] = wm.reshape(DIM, HEADS, HD)
    w[DIM, :, :HD] = bm.reshape(HEADS, HD)
    w[DIM, :, HD] = 1.0
    return w.reshape(DIM + 4, HEADS * VW)


def kernel(**inputs):
    import concourse.bacc as bacc
    from concourse.bass_utils import run_bass_kernel_spmd

    a = {k: np.asarray(v) for k, v in inputs.items()}
    qkv_w = a["L0_ffn_qkv_w"].reshape(DIM, 3, DIM)
    qkv_b = a["L0_ffn_qkv_b"].reshape(3, DIM)
    qk = np.stack([_slots(a["L0_attn_Wq"].T, a["L0_attn_bq"], a["L0_attn_Wk"].T, a["L0_attn_bk"]),
                   _slots(qkv_w[:, 0], qkv_b[0], qkv_w[:, 1], qkv_b[1])])
    vv = np.stack([_values(a["L0_attn_Wv"].T, a["L0_attn_bv"]), _values(qkv_w[:, 2], qkv_b[2])])

    def ln(g, b):
        w = np.zeros((P, 4), np.float32)
        w[:, 0], w[:, 1] = g[:P], b[:P]
        w[:D1, 2], w[:D1, 3] = g[P:], b[P:]
        return w

    token = np.arange(NT)[None] * TT + np.arange(TT)[:, None]
    real = (token < IMAGES * TOK).astype(np.float32)
    route = np.concatenate([
        np.tile(np.arange(EXPERTS), (TT, NT)), np.tile(np.arange(MAXT) * ST, (TT, EXPERTS)),
        np.tile((np.arange(EXPERTS)[None] < np.arange(EXPERTS)[:, None]).reshape(1, -1), (TT, 1)),
        np.tile(np.repeat(np.arange(NS), EXPERTS)[None], (TT, 1)),
        token - OUTSIDE, token + NT * TT - OUTSIDE, (1 - real) * OUTSIDE, real, np.ones((TT, NT)),
    ], axis=1).astype(np.float32)
    tri = np.stack([np.triu(np.ones((TT, TT), np.float32), 1), np.ones((TT, TT), np.float32)], axis=1)
    keep_low = np.zeros((P, 2), np.float32)
    keep_low[:, 0] = W1S
    keep_low[D1, 0] = 0.0
    keep_low[1, 1] = W2S
    aug = np.zeros((4, NT * TT), np.float32)
    aug[0] = 1.0
    for i in range(TI):
        aug[1 + i] = np.tile(np.repeat(np.arange(TI) == i, TOK), NT)
    pt = a["x"].reshape(IMAGES, CHANNELS, PER_SIDE, PATCH, PER_SIDE, PATCH).transpose(0, 1, 2, 4, 3, 5)
    px = np.zeros((NT * TI, TOK, PIX), np.float32)
    px[:IMAGES, 1:] = pt.reshape(IMAGES, PATCHES, PIX)
    px = px.reshape(NG, GT, TT, KC, P).transpose(0, 4, 1, 3, 2).reshape(NG, P, GT * KC * TT)
    arrays = {
        "x": px, "pos": a["L0_tok_pos_embedding"],
        "tok_b": np.repeat(a["L0_tok_b"].reshape(1, DIM), TT, 0), "cls": a["L0_tok_class_token"],
        "w_emb": a["L0_tok_W"].T,
        "wqk_a": qk[:, :P], "wqk_b": qk[:, P:], "wv_a": vv[:, :P], "wv_b": vv[:, P:],
        "ln1": ln(a["L0_ffn_ln1_g"], a["L0_ffn_ln1_b"]),
        "ln2_g": np.repeat(a["L0_ffn_ln2_g"].reshape(1, DIM), TT, 0),
        "ln2_b": np.repeat(a["L0_ffn_ln2_b"].reshape(1, DIM), TT, 0),
        "proj": np.concatenate([a["L0_ffn_proj_w"], a["L0_ffn_proj_b"].reshape(1, DIM)]),
        "gate": a["L0_ffn_gate_w"], "w1": a["L0_ffn_w1"], "b1": a["L0_ffn_b1"],
        "w2": a["L0_ffn_w2"], "b2": a["L0_ffn_b2"],
        "ident": np.eye(P, dtype=np.float32), "aug": aug,
        "route": route, "tri": tri, "keep": keep_low,
    }
    arrays = {k: np.ascontiguousarray(v) for k, v in arrays.items()}
    nc = bacc.Bacc("TRN2", target_bir_lowering=False, num_devices=1)
    args = [nc.dram_tensor(f"in_{k}", v.shape, mybir.dt.from_np(v.dtype), kind="ExternalInput").ap()
            for k, v in arrays.items()]
    args.append(nc.dram_tensor("slots", (NSLOT, XW), mybir.dt.float32, kind="Internal").ap())
    args.append(nc.dram_tensor("ymoe", (2 * NT * TT, DIM), mybir.dt.float32, kind="Internal").ap())
    out = nc.dram_tensor("out", (NT, TT, DIM), mybir.dt.float32, kind="ExternalOutput").ap()
    build(nc, *args, out)
    r = run_bass_kernel_spmd(nc, [{f"in_{k}": v for k, v in arrays.items()}], core_ids=[0])
    return r.results[0]["out"].reshape(NT * TT, DIM)[:IMAGES * TOK].reshape(IMAGES, TOK, DIM)
```
